# Optimizing a Trainium2 kernel written in Bass

```python
import numpy as np
import jax
import jax.numpy as jnp

def _softmax(x, axis=-1):
    return jax.nn.softmax(x, axis=axis)

def _gelu(x):
    return jax.nn.gelu(x, approximate=True)

def _silu(x):
    return jax.nn.silu(x)

def _sigmoid(x):
    return jax.nn.sigmoid(x)

def _layernorm(x, axis=-1, eps=1e-05):
    m = jnp.mean(x, axis=axis, keepdims=True)
    v = jnp.var(x, axis=axis, keepdims=True)
    return (x - m) / jnp.sqrt(v + eps)

def _scatter_add(tgt, idx, src, axis=0):
    return tgt.at[idx].add(src)

def _segment_sum(src, seg, n):
    return jax.ops.segment_sum(src, seg, n)
kernel_name = 'mk_xattn_ffn_d4_seqx_r4_e49ff5'

def setup_inputs(seed: int=0):
    np.random.seed(seed)
    _w = jnp.asarray

    def _rec_inputs():
        import jax
        import jax.numpy as jnp
        _rk = jax.random.key(seed)
        x = -0.0003929 + 0.9999 * jax.random.normal(jax.random.fold_in(_rk, 1), (8, 256, 256), jnp.float32)
        _lenS = 256 - jax.random.randint(jax.random.fold_in(_rk, 7), (8,), 0, max(1, 256 // 4) + 1, jnp.int32)
        _lenS2 = 256 - jax.random.randint(jax.random.fold_in(_rk, 8), (8,), 0, max(1, 256 // 4) + 1, jnp.int32)
        _ctx_2048P = jax.random.normal(jax.random.fold_in(_rk, 11), (8, 16, 512), jnp.float32)
        _ctx_2048c = jax.random.dirichlet(jax.random.fold_in(_rk, 511), 0.3 * jnp.ones((16,), jnp.float32), (8, 256))
        _ctx_2048t = jnp.einsum('bsk,bkd->bsd', _ctx_2048c, _ctx_2048P)
        _ctx_2048t = _ctx_2048t * jax.lax.rsqrt(jnp.mean(jnp.square(_ctx_2048t)) + 1e-12) * 0.953939
        ctx_2048 = 4.13588e-05 + 0.999923 * (_ctx_2048t + 0.3 * jax.random.normal(jax.random.fold_in(_rk, 611), (8, 256, 512), jnp.float32))
        _validS = jnp.arange(256)[None, :] < _lenS[:, None]
        _validS2 = jnp.arange(256)[None, :] < _lenS2[:, None]
        _causal = jnp.tril(jnp.ones((256, 256), dtype=bool))
        mask_BxS2_if0 = jnp.where(jnp.ones((8, 256), dtype=bool), 4, 0).astype(jnp.int32)
        mask_BxS2_fk1 = jnp.where(jnp.broadcast_to(_validS2[:, :], (8, 256)), 1.0, 0.0).astype(jnp.float32)
        return (x, ctx_2048, mask_BxS2_if0, mask_BxS2_fk1)
    x, ctx_2048, mask_BxS2_if0, mask_BxS2_fk1 = _rec_inputs()

    def _L0_xattn_setup():
        import jax, jax.numpy as jnp
        import numpy as np
        B, L, P = (4, 1024, 256)
        D_MODEL = 256
        D_GLOBAL = 512
        HEADDIM = 32
        EPSILON = 0.001
        RMS_EPS = 1e-05

        def rmsnorm(x, g, eps=RMS_EPS):
            var = jnp.mean(jnp.square(x), axis=-1, keepdims=True)
            return x * jax.lax.rsqrt(var + eps) * g

        def _hnet_depool(h, h_patch_full, patch_lens):
            h_patch = h_patch_full[..., :D_MODEL]
            bsz, plen = (h_patch.shape[0], h_patch.shape[1])
            seqlen = h.shape[1]
            logp = jnp.full((bsz, plen), -EPSILON, dtype=jnp.float32)
            bidx = jnp.cumsum(patch_lens, axis=1) - 1
            boundary_mask = jnp.zeros((bsz, seqlen), dtype=jnp.int32)
            boundary_mask = boundary_mask.at[jnp.arange(bsz)[:, None], bidx].set(1)
            dt = (-jnp.log(-jnp.expm1(logp))).astype(h_patch.dtype)
            x = h_patch / dt[..., None]
            n_heads = D_MODEL // HEADDIM
            A = -jnp.ones((n_heads,), dtype=jnp.float32)
            bcoef = jnp.exp(logp).astype(h_patch.dtype)
            x4 = x.reshape(bsz, plen, n_heads, HEADDIM)
            a = jnp.exp(dt[:, :, None] * A[None, None, :])
            u = (dt * bcoef)[:, :, None, None] * x4
            a_b = jnp.broadcast_to(a[..., None], u.shape)

            def comb(lft, rgt):
                aL, uL = lft
                aR, uR = rgt
                return (aL * aR, uL * aR + uR)
            _, s = jax.lax.associative_scan(comb, (a_b, u), axis=1)
            depool = s.reshape(bsz, plen, D_MODEL)
            plug = jnp.clip(jnp.cumsum(boundary_mask, axis=1) - 1, 0, plen - 1)
            depool_out = depool[jnp.arange(bsz)[:, None], plug]
            return depool_out + h
        key = jax.random.key(seed)
        k1, k2, k3, k4 = jax.random.split(key, 4)
        embeds = jax.random.normal(k1, (B, L, D_MODEL), dtype=jnp.float32)
        patch_embeds = jax.random.normal(k2, (B, P, D_GLOBAL), dtype=jnp.float32)
        patch_lens = jnp.full((B, P), L // P, dtype=jnp.int64)
        W_in = jax.random.normal(k3, (D_MODEL, D_MODEL), dtype=jnp.float32) * 0.02
        b_in = jnp.zeros((D_MODEL,), dtype=jnp.float32)
        g_res = jnp.ones((D_MODEL,), dtype=jnp.float32)
        g_init = jnp.ones((D_GLOBAL,), dtype=jnp.float32)
        return {'embeds': embeds, 'patch_embeds': patch_embeds, 'patch_lens': patch_lens, 'W_in': W_in, 'b_in': b_in, 'g_res': g_res, 'g_init': g_init}
    _L0_xattn_all = _L0_xattn_setup()
    _L0_xattn_in = {k: v for k, v in _L0_xattn_all.items() if k in ('W_in', 'b_in', 'g_res', 'g_init')}
    del _L0_xattn_all

    def _L0_ffn_setup():
        import jax, jax.numpy as jnp
        import numpy as np
        B, N, C, H, REG = (1, 2309, 256, 16, 5)
        D = C // H
        key = jax.random.key(seed)
        k0, k1, k2, k3 = jax.random.split(key, 4)
        x = jax.random.normal(k0, (B, N, C), dtype=jnp.float32)
        g_info = jax.random.normal(k1, (12, 2, C), dtype=jnp.float32)
        W_qkv = jax.random.normal(k2, (C, 3 * C), dtype=jnp.float32) * 0.02
        W_proj = jax.random.normal(k3, (C, C), dtype=jnp.float32) * 0.02
        b_proj = jnp.zeros((C,), dtype=jnp.float32)
        return {'x': x, 'g_info': g_info, 'W_qkv': W_qkv, 'W_proj': W_proj, 'b_proj': b_proj}
    _L0_ffn_all = _L0_ffn_setup()
    _L0_ffn_in = {k: v for k, v in _L0_ffn_all.items() if k in ('g_info', 'W_qkv', 'W_proj', 'b_proj')}
    del _L0_ffn_all

    def _L1_xattn_setup():
        import jax, jax.numpy as jnp
        import numpy as np
        NUM_HEADS = 16
        key = jax.random.key(seed)
        ks = jax.random.split(key, 5)
        dim = 256
        B, N, N_c = (4, 256, 64)
        x = jax.random.normal(ks[0], (B, N, dim), dtype=jnp.float32)
        context = jax.random.normal(ks[1], (B, N_c, 2 * dim), dtype=jnp.float32)
        w_qkv = jax.random.normal(ks[2], (3 * dim, dim), dtype=jnp.float32) * 0.02
        w_proj = jax.random.normal(ks[3], (dim, dim), dtype=jnp.float32) * 0.02
        b_proj = jax.random.normal(ks[4], (dim,), dtype=jnp.float32) * 0.02
        return {'x': x, 'context': context, 'w_qkv': w_qkv, 'w_proj': w_proj, 'b_proj': b_proj}
    _L1_xattn_all = _L1_xattn_setup()
    _L1_xattn_in = {k: v for k, v in _L1_xattn_all.items() if k in ('w_qkv', 'w_proj', 'b_proj')}
    del _L1_xattn_all

    def _L1_ffn_setup():
        import jax, jax.numpy as jnp
        import numpy as np
        N_EMBD = 256
        EXPERT_SIZES = [(4, 256), (4, 512)]
        TOP_K = 2
        B, S = (1, 512)
        WIDTHS = []
        for count, size in EXPERT_SIZES:
            WIDTHS += [size] * count
        OFFSETS = np.concatenate([[0], np.cumsum(WIDTHS)]).astype(np.int64)
        E = len(WIDTHS)
        TOTAL_W = int(OFFSETS[-1])
        MAX_W = max(WIDTHS)

        def _stack_experts(w1, w2):
            W1e, W2e = ([], [])
            for e in range(E):
                off, wd = (int(OFFSETS[e]), WIDTHS[e])
                pad = MAX_W - wd
                W1e.append(jnp.pad(w1[:, off:off + wd], ((0, 0), (0, pad))))
                W2e.append(jnp.pad(w2[off:off + wd, :], ((0, pad), (0, 0))))
            return (jnp.stack(W1e), jnp.stack(W2e))
        key = jax.random.key(seed)
        k1, k2, k3, k4 = jax.random.split(key, 4)
        x = jax.random.normal(k1, (B, S, N_EMBD), jnp.float32)
        router_w = jax.random.normal(k2, (E, N_EMBD), jnp.float32) * 0.02
        w1 = jax.random.truncated_normal(k3, -3.0, 3.0, (N_EMBD, TOTAL_W), jnp.float32) * 0.02
        w2 = jax.random.truncated_normal(k4, -3.0, 3.0, (TOTAL_W, N_EMBD), jnp.float32) * 0.02
        return {'x': x, 'router_w': router_w, 'w1': w1, 'w2': w2}
    _L1_ffn_all = _L1_ffn_setup()
    _L1_ffn_in = {k: v for k, v in _L1_ffn_all.items() if k in ('router_w', 'w1', 'w2')}
    del _L1_ffn_all

    def _L2_xattn_setup():
        import jax, jax.numpy as jnp
        import numpy as np
        B, N, DIM = (8, 1024, 256)
        M, CTX = (64, 512)
        HEADS, DH = (16, 64)
        INNER = HEADS * DH
        EPS = 1e-06

        def _split_heads(t):
            b, n, _ = t.shape
            return t.reshape(b, n, HEADS, DH).transpose(0, 2, 1, 3)
        key = jax.random.key(seed)
        ks = jax.random.split(key, 6)
        x = jax.random.normal(ks[0], (B, N, DIM), dtype=jnp.float32)
        context = jax.random.normal(ks[1], (B, M, CTX), dtype=jnp.float32)
        Wq = jax.random.normal(ks[2], (DIM, INNER), dtype=jnp.float32) / np.sqrt(DIM)
        Wkv = jax.random.normal(ks[3], (CTX, 2 * INNER), dtype=jnp.float32) / np.sqrt(CTX)
        null_kv = jax.random.normal(ks[4], (2, DH), dtype=jnp.float32) / np.sqrt(2.0)
        Wout = jax.random.normal(ks[5], (INNER, DIM), dtype=jnp.float32) / np.sqrt(INNER)
        ln_scale = jnp.ones((DIM,), dtype=jnp.float32)
        ln_bias = jnp.zeros((DIM,), dtype=jnp.float32)
        return {'x': x, 'context': context, 'Wq': Wq, 'Wkv': Wkv, 'null_kv': null_kv, 'Wout': Wout, 'ln_scale': ln_scale, 'ln_bias': ln_bias}
    _L2_xattn_all = _L2_xattn_setup()
    _L2_xattn_in = {k: v for k, v in _L2_xattn_all.items() if k in ('Wq', 'Wkv', 'null_kv', 'Wout', 'ln_scale', 'ln_bias')}
    del _L2_xattn_all

    def _L2_ffn_setup():
        import jax, jax.numpy as jnp
        import numpy as np
        import math
        D_IN = 256
        FEATURES = (1024, 1024, 256)
        BATCH, SEQ = (8, 512)

        def _conn_dense(kernel_bool, x):
            w = jnp.where(kernel_bool, jnp.float32(1.0), jnp.float32(-1.0))
            return x @ w
        key = jax.random.key(seed)
        kx, kk0, kk1, kk2 = jax.random.split(key, 4)
        x = jax.random.normal(kx, (BATCH, SEQ, D_IN), dtype=jnp.float32)
        k0 = jax.random.randint(kk0, (2 * D_IN, FEATURES[0]), 0, 2).astype(jnp.bool_)
        k1 = jax.random.randint(kk1, (FEATURES[0], FEATURES[1]), 0, 2).astype(jnp.bool_)
        k2 = jax.random.randint(kk2, (FEATURES[1], FEATURES[2]), 0, 2).astype(jnp.bool_)
        s0 = jnp.asarray(1.0 / math.sqrt(2 * D_IN), dtype=jnp.float32)
        s1 = jnp.asarray(1.0 / math.sqrt(FEATURES[0]), dtype=jnp.float32)
        s2 = jnp.asarray(1.0 / math.sqrt(FEATURES[1]), dtype=jnp.float32)
        return {'x': x, 'k0': k0, 'k1': k1, 'k2': k2, 's0': s0, 's1': s1, 's2': s2}
    _L2_ffn_all = _L2_ffn_setup()
    _L2_ffn_in = {k: v for k, v in _L2_ffn_all.items() if k in ('k0', 'k1', 'k2', 's0', 's1', 's2')}
    del _L2_ffn_all

    def _L3_xattn_setup():
        import jax, jax.numpy as jnp
        import numpy as np
        B, S, T = (32, 128, 128)
        SRC_SIZE, TGT_SIZE, OUT_SIZE, NUM_HEAD = (512, 256, 256, 8)
        HEAD_DIM = OUT_SIZE // NUM_HEAD
        key = jax.random.key(seed)
        ks = jax.random.split(key, 12)
        src = jax.random.normal(ks[0], (B, S, SRC_SIZE), dtype=jnp.float32)
        tgt = jax.random.normal(ks[1], (B, T, TGT_SIZE), dtype=jnp.float32)
        src_mask = (jax.random.uniform(ks[2], (B, S)) > 0.3).astype(jnp.float32)
        src_mask = src_mask.at[:, 0].set(1.0)
        tgt_mask = (jax.random.uniform(ks[3], (B, T)) > 0.3).astype(jnp.float32)
        tgt_mask = tgt_mask.at[:, 0].set(1.0)

        def lin(k, out_f, in_f):
            return jax.random.normal(k, (out_f, in_f), dtype=jnp.float32) / np.sqrt(in_f)
        W_src = lin(ks[4], 2 * OUT_SIZE, SRC_SIZE)
        b_src = jnp.zeros((2 * OUT_SIZE,), jnp.float32)
        W_tgt = lin(ks[5], OUT_SIZE, TGT_SIZE)
        b_tgt = jnp.zeros((OUT_SIZE,), jnp.float32)
        W_out = lin(ks[6], OUT_SIZE, OUT_SIZE + TGT_SIZE)
        b_out = jnp.zeros((OUT_SIZE,), jnp.float32)
        return {'src': src, 'tgt': tgt, 'src_mask': src_mask, 'tgt_mask': tgt_mask, 'W_src': W_src, 'b_src': b_src, 'W_tgt': W_tgt, 'b_tgt': b_tgt, 'W_out': W_out, 'b_out': b_out}
    _L3_xattn_all = _L3_xattn_setup()
    _L3_xattn_in = {k: v for k, v in _L3_xattn_all.items() if k in ('W_src', 'b_src', 'W_tgt', 'b_tgt', 'W_out', 'b_out')}
    del _L3_xattn_all

    def _L3_ffn_setup():
        import jax, jax.numpy as jnp
        import numpy as np
        D = 256
        H = 4
        HD = D // H
        E = 8
        FF = 1024
        CAP_FACTOR = 1.0

        def _ln(x, g, b, eps=1e-05):
            mu = jnp.mean(x, -1, keepdims=True)
            v = jnp.mean((x - mu) ** 2, -1, keepdims=True)
            return (x - mu) * jax.lax.rsqrt(v + eps) * g + b

        def _mha(x, w, b, ow, ob):
            L, N, _ = x.shape
            qkv = x @ w.T + b
            q, k, v = jnp.split(qkv, 3, axis=-1)
            rh = lambda t: t.reshape(L, N, H, HD).transpose(1, 2, 0, 3)
            q, k, v = (rh(q), rh(k), rh(v))
            scores = jnp.einsum('nhld,nhmd->nhlm', q, k) / np.float32(np.sqrt(HD))
            attn = jax.nn.softmax(scores, axis=-1)
            o = jnp.einsum('nhlm,nhmd->nhld', attn, v).transpose(2, 0, 1, 3).reshape(L, N, D)
            return o @ ow.T + ob

        def _moe(x, wg, w1, b1, w2, b2):
            L, N, _ = x.shape
            S = L * N
            cap = int(CAP_FACTOR * S) // E
            xf = x.reshape(S, D)
            gates = jax.nn.softmax(xf @ wg, axis=-1)
            idx = jnp.argmax(gates, axis=-1)
            mask1 = jax.nn.one_hot(idx, E, dtype=x.dtype)
            loc = jnp.sum((jnp.cumsum(mask1, 0) - 1.0) * mask1, -1).astype(jnp.int32)
            keep = loc < cap
            gate_val = jnp.take_along_axis(gates, idx[:, None], -1)[:, 0]
            slot = jnp.where(keep, idx.astype(jnp.int32) * cap + loc, E * cap)
            disp = jnp.zeros((E * cap, D), x.dtype).at[slot].set(xf, mode='drop')
            disp = disp.reshape(E, cap, D)
            h = jnp.einsum('ecd,edf->ecf', disp, w1) + b1[:, None, :]
            y = (jnp.einsum('ecf,efd->ecd', h, w2) + b2[:, None, :]).reshape(E * cap, D)
            out = jnp.where(keep[:, None], gate_val[:, None] * y[jnp.minimum(slot, E * cap - 1)], 0.0)
            return out.reshape(L, N, D)
        key = jax.random.key(seed)
        ks = jax.random.split(key, 8)
        L, N = (256, 16)
        s = 0.02
        return {'x': jax.random.normal(ks[0], (L, N, D), jnp.float32), 'in_proj_w': jax.random.normal(ks[1], (3 * D, D), jnp.float32) * s, 'in_proj_b': jnp.zeros((3 * D,), jnp.float32), 'out_proj_w': jax.random.normal(ks[2], (D, D), jnp.float32) * s, 'out_proj_b': jnp.zeros((D,), jnp.float32), 'ln1_g': jnp.ones((D,), jnp.float32), 'ln1_b': jnp.zeros((D,), jnp.float32), 'ln2_g': jnp.ones((D,), jnp.float32), 'ln2_b': jnp.zeros((D,), jnp.float32), 'wg': jax.random.normal(ks[3], (D, E), jnp.float32) * s, 'w1': jax.random.normal(ks[4], (E, D, FF), jnp.float32) * s, 'b1': jnp.zeros((E, FF), jnp.float32), 'w2': jax.random.normal(ks[5], (E, FF, D), jnp.float32) * s, 'b2': jnp.zeros((E, D), jnp.float32)}
    _L3_ffn_all = _L3_ffn_setup()
    _L3_ffn_in = {k: v for k, v in _L3_ffn_all.items() if k in ('in_proj_w', 'in_proj_b', 'out_proj_w', 'out_proj_b', 'ln1_g', 'ln1_b', 'ln2_g', 'ln2_b', 'wg', 'w1', 'b1', 'w2', 'b2')}
    del _L3_ffn_all
    return {'x': x, 'ctx_2048': ctx_2048, 'mask_BxS2_if0': mask_BxS2_if0, 'mask_BxS2_fk1': mask_BxS2_fk1, 'L0_xattn_W_in': _L0_xattn_in['W_in'], 'L0_xattn_b_in': _L0_xattn_in['b_in'], 'L0_xattn_g_res': _L0_xattn_in['g_res'], 'L0_xattn_g_init': _L0_xattn_in['g_init'], 'L0_ffn_g_info': _L0_ffn_in['g_info'], 'L0_ffn_W_qkv': _L0_ffn_in['W_qkv'], 'L0_ffn_W_proj': _L0_ffn_in['W_proj'], 'L0_ffn_b_proj': _L0_ffn_in['b_proj'], 'L1_xattn_w_qkv': _L1_xattn_in['w_qkv'], 'L1_xattn_w_proj': _L1_xattn_in['w_proj'], 'L1_xattn_b_proj': _L1_xattn_in['b_proj'], 'L1_ffn_router_w': _L1_ffn_in['router_w'], 'L1_ffn_w1': _L1_ffn_in['w1'], 'L1_ffn_w2': _L1_ffn_in['w2'], 'L2_xattn_Wq': _L2_xattn_in['Wq'], 'L2_xattn_Wkv': _L2_xattn_in['Wkv'], 'L2_xattn_null_kv': _L2_xattn_in['null_kv'], 'L2_xattn_Wout': _L2_xattn_in['Wout'], 'L2_xattn_ln_scale': _L2_xattn_in['ln_scale'], 'L2_xattn_ln_bias': _L2_xattn_in['ln_bias'], 'L2_ffn_k0': _L2_ffn_in['k0'], 'L2_ffn_k1': _L2_ffn_in['k1'], 'L2_ffn_k2': _L2_ffn_in['k2'], 'L2_ffn_s0': _L2_ffn_in['s0'], 'L2_ffn_s1': _L2_ffn_in['s1'], 'L2_ffn_s2': _L2_ffn_in['s2'], 'L3_xattn_W_src': _L3_xattn_in['W_src'], 'L3_xattn_b_src': _L3_xattn_in['b_src'], 'L3_xattn_W_tgt': _L3_xattn_in['W_tgt'], 'L3_xattn_b_tgt': _L3_xattn_in['b_tgt'], 'L3_xattn_W_out': _L3_xattn_in['W_out'], 'L3_xattn_b_out': _L3_xattn_in['b_out'], 'L3_ffn_in_proj_w': _L3_ffn_in['in_proj_w'], 'L3_ffn_in_proj_b': _L3_ffn_in['in_proj_b'], 'L3_ffn_out_proj_w': _L3_ffn_in['out_proj_w'], 'L3_ffn_out_proj_b': _L3_ffn_in['out_proj_b'], 'L3_ffn_ln1_g': _L3_ffn_in['ln1_g'], 'L3_ffn_ln1_b': _L3_ffn_in['ln1_b'], 'L3_ffn_ln2_g': _L3_ffn_in['ln2_g'], 'L3_ffn_ln2_b': _L3_ffn_in['ln2_b'], 'L3_ffn_wg': _L3_ffn_in['wg'], 'L3_ffn_w1': _L3_ffn_in['w1'], 'L3_ffn_b1': _L3_ffn_in['b1'], 'L3_ffn_w2': _L3_ffn_in['w2'], 'L3_ffn_b2': _L3_ffn_in['b2']}

def reference(x, ctx_2048, mask_BxS2_if0, mask_BxS2_fk1, L0_xattn_W_in, L0_xattn_b_in, L0_xattn_g_res, L0_xattn_g_init, L0_ffn_g_info, L0_ffn_W_qkv, L0_ffn_W_proj, L0_ffn_b_proj, L1_xattn_w_qkv, L1_xattn_w_proj, L1_xattn_b_proj, L1_ffn_router_w, L1_ffn_w1, L1_ffn_w2, L2_xattn_Wq, L2_xattn_Wkv, L2_xattn_null_kv, L2_xattn_Wout, L2_xattn_ln_scale, L2_xattn_ln_bias, L2_ffn_k0, L2_ffn_k1, L2_ffn_k2, L2_ffn_s0, L2_ffn_s1, L2_ffn_s2, L3_xattn_W_src, L3_xattn_b_src, L3_xattn_W_tgt, L3_xattn_b_tgt, L3_xattn_W_out, L3_xattn_b_out, L3_ffn_in_proj_w, L3_ffn_in_proj_b, L3_ffn_out_proj_w, L3_ffn_out_proj_b, L3_ffn_ln1_g, L3_ffn_ln1_b, L3_ffn_ln2_g, L3_ffn_ln2_b, L3_ffn_wg, L3_ffn_w1, L3_ffn_b1, L3_ffn_w2, L3_ffn_b2):
    import jax
    import jax.numpy as jnp

    def _L0_xattn_ref(embeds, patch_embeds, patch_lens, W_in, b_in, g_res, g_init):
        import jax, jax.numpy as jnp
        import numpy as np
        B, L, P = (4, 1024, 256)
        D_MODEL = 256
        D_GLOBAL = 512
        HEADDIM = 32
        EPSILON = 0.001
        RMS_EPS = 1e-05

        def rmsnorm(x, g, eps=RMS_EPS):
            var = jnp.mean(jnp.square(x), axis=-1, keepdims=True)
            return x * jax.lax.rsqrt(var + eps) * g

        def _hnet_depool(h, h_patch_full, patch_lens):
            h_patch = h_patch_full[..., :D_MODEL]
            bsz, plen = (h_patch.shape[0], h_patch.shape[1])
            seqlen = h.shape[1]
            logp = jnp.full((bsz, plen), -EPSILON, dtype=jnp.float32)
            bidx = jnp.cumsum(patch_lens, axis=1) - 1
            boundary_mask = jnp.zeros((bsz, seqlen), dtype=jnp.int32)
            boundary_mask = boundary_mask.at[jnp.arange(bsz)[:, None], bidx].set(1)
            dt = (-jnp.log(-jnp.expm1(logp))).astype(h_patch.dtype)
            x = h_patch / dt[..., None]
            n_heads = D_MODEL // HEADDIM
            A = -jnp.ones((n_heads,), dtype=jnp.float32)
            bcoef = jnp.exp(logp).astype(h_patch.dtype)
            x4 = x.reshape(bsz, plen, n_heads, HEADDIM)
            a = jnp.exp(dt[:, :, None] * A[None, None, :])
            u = (dt * bcoef)[:, :, None, None] * x4
            a_b = jnp.broadcast_to(a[..., None], u.shape)

            def comb(lft, rgt):
                aL, uL = lft
                aR, uR = rgt
                return (aL * aR, uL * aR + uR)
            _, s = jax.lax.associative_scan(comb, (a_b, u), axis=1)
            depool = s.reshape(bsz, plen, D_MODEL)
            plug = jnp.clip(jnp.cumsum(boundary_mask, axis=1) - 1, 0, plen - 1)
            depool_out = depool[jnp.arange(bsz)[:, None], plug]
            return depool_out + h
        h = rmsnorm(embeds, g_res)
        h = jnp.einsum('bld,ed->ble', h, W_in) + b_in
        h_patch = rmsnorm(patch_embeds, g_init)
        return _hnet_depool(h, h_patch, patch_lens)

    def _L0_ffn_ref(x, g_info, W_qkv, W_proj, b_proj):
        import jax, jax.numpy as jnp
        import numpy as np
        B, N, C, H, REG = (1, 2309, 256, 16, 5)
        D = C // H
        Bx, Nx, Cx = x.shape
        scale = D ** (-0.5)
        qkv = (x @ W_qkv).reshape(Bx, Nx, 3, H, D)
        q, k, v = (qkv[:, :, 0], qkv[:, :, 1], qkv[:, :, 2])
        g_layer = g_info[0].reshape(-1, H, D)
        q_g = g_layer[0]
        q_pure = q[:, REG:]
        q_n = q_pure / jnp.linalg.norm(q_pure, axis=-1, keepdims=True)
        qg_n = q_g / jnp.linalg.norm(q_g, axis=-1, keepdims=True)
        sim = (qg_n[None, None] * q_n).sum(-1).mean(-1)
        sim = (sim - sim.min()) / (sim.max() - sim.min())
        pos = sim > 0.9
        logits = jnp.einsum('bqhd,bkhd->bhqk', q * scale, k)

        def masked_attn(tok_mask):
            key_mask = jnp.concatenate([jnp.ones((Bx, REG), bool), tok_mask], axis=1)
            l = jnp.where(key_mask[:, None, None, :], logits, -jnp.inf)
            a = jax.nn.softmax(l, axis=-1)
            return jnp.einsum('bhqk,bkhd->bqhd', a, v)
        x_pos = masked_attn(pos)
        x_neg = masked_attn(~pos)
        reg_out = (x_pos[:, :REG] + x_neg[:, :REG]) * 0.5
        tok_out = jnp.where(pos[:, :, None, None], x_pos[:, REG:], x_neg[:, REG:])
        out = jnp.concatenate([reg_out, tok_out], axis=1).reshape(Bx, Nx, Cx)
        return out @ W_proj + b_proj

    def _L1_xattn_ref(x, context, w_qkv, w_proj, b_proj):
        import jax, jax.numpy as jnp
        import numpy as np
        NUM_HEADS = 16
        B, N, C = x.shape
        H = NUM_HEADS
        D = C // H
        scale = D ** (-0.5)
        qkv = (x @ w_qkv.T).reshape(B, N, 3, H, D).transpose(2, 0, 3, 1, 4)
        q, k, v = (qkv[0], qkv[1], qkv[2])
        N_c = context.shape[1]
        kv = context.reshape(B, N_c, 2, H, D).transpose(2, 0, 3, 1, 4)
        extra_k, extra_v = (kv[0], kv[1])
        k = jnp.concatenate([extra_k, k], axis=2)
        v = jnp.concatenate([extra_v, v], axis=2)
        dtype = q.dtype
        attn = jnp.einsum('bhnd,bhmd->bhnm', q * scale, k).astype(jnp.float32)
        attn = jax.nn.softmax(attn, axis=-1).astype(dtype)
        out = jnp.einsum('bhnm,bhmd->bhnd', attn, v)
        out = out.transpose(0, 2, 1, 3).reshape(B, N, C)
        return out @ w_proj.T + b_proj

    def _L1_ffn_ref(x, router_w, w1, w2):
        import jax, jax.numpy as jnp
        import numpy as np
        N_EMBD = 256
        EXPERT_SIZES = [(4, 256), (4, 512)]
        TOP_K = 2
        B, S = (1, 512)
        WIDTHS = []
        for count, size in EXPERT_SIZES:
            WIDTHS += [size] * count
        OFFSETS = np.concatenate([[0], np.cumsum(WIDTHS)]).astype(np.int64)
        E = len(WIDTHS)
        TOTAL_W = int(OFFSETS[-1])
        MAX_W = max(WIDTHS)

        def _stack_experts(w1, w2):
            W1e, W2e = ([], [])
            for e in range(E):
                off, wd = (int(OFFSETS[e]), WIDTHS[e])
                pad = MAX_W - wd
                W1e.append(jnp.pad(w1[:, off:off + wd], ((0, 0), (0, pad))))
                W2e.append(jnp.pad(w2[off:off + wd, :], ((0, pad), (0, 0))))
            return (jnp.stack(W1e), jnp.stack(W2e))
        b, s, d = x.shape
        xf = x.reshape(-1, d)
        logits = xf @ router_w.T
        probs = jax.nn.sigmoid(logits.astype(jnp.float32))
        topw, sel = jax.lax.top_k(probs, TOP_K)
        topw = topw / (topw.sum(-1, keepdims=True) + 1e-20)
        topw = topw.astype(x.dtype)
        onehot = sel[:, :, None] == jnp.arange(E)[None, None, :]
        combine = jnp.sum(topw[:, :, None] * onehot, axis=1)
        W1e, W2e = _stack_experts(w1, w2)
        h = jnp.einsum('td,edw->tew', xf, W1e)
        h = jnp.square(jax.nn.relu(h))
        y = jnp.einsum('tew,ewd->ted', h, W2e)
        out = jnp.einsum('ted,te->td', y, combine)
        return out.reshape(b, s, d)

    def _L2_xattn_ref(x, context, Wq, Wkv, null_kv, Wout, ln_scale, ln_bias):
        import jax, jax.numpy as jnp
        import numpy as np
        B, N, DIM = (8, 1024, 256)
        M, CTX = (64, 512)
        HEADS, DH = (16, 64)
        INNER = HEADS * DH
        EPS = 1e-06

        def _split_heads(t):
            b, n, _ = t.shape
            return t.reshape(b, n, HEADS, DH).transpose(0, 2, 1, 3)
        scale = DH ** (-0.5)
        b = x.shape[0]
        q = _split_heads(jnp.einsum('bnd,df->bnf', x, Wq))
        kv = jnp.einsum('bmc,cf->bmf', context, Wkv)
        k, v = jnp.split(kv, 2, axis=-1)
        k, v = (_split_heads(k), _split_heads(v))
        nk = jnp.broadcast_to(null_kv[0], (b, HEADS, 1, DH))
        nv = jnp.broadcast_to(null_kv[1], (b, HEADS, 1, DH))
        k = jnp.concatenate((nk, k), axis=-2)
        v = jnp.concatenate((nv, v), axis=-2)
        q = q * scale
        sim = jnp.einsum('bhid,bhjd->bhij', q, k)
        attn = jax.nn.softmax(sim, axis=-1)
        out = jnp.einsum('bhij,bhjd->bhid', attn, v)
        out = out.transpose(0, 2, 1, 3).reshape(b, -1, INNER)
        out = jnp.einsum('bnf,fd->bnd', out, Wout)
        mu = jnp.mean(out, axis=-1, keepdims=True)
        var = jnp.var(out, axis=-1, keepdims=True)
        out = (out - mu) * jax.lax.rsqrt(var + EPS) * ln_scale + ln_bias
        return out

    def _L2_ffn_ref(x, k0, k1, k2, s0, s1, s2):
        import jax, jax.numpy as jnp
        import numpy as np
        import math
        D_IN = 256
        FEATURES = (1024, 1024, 256)
        BATCH, SEQ = (8, 512)

        def _conn_dense(kernel_bool, x):
            w = jnp.where(kernel_bool, jnp.float32(1.0), jnp.float32(-1.0))
            return x @ w
        h = jnp.concatenate([x, -x], axis=-1)
        h = s0 * _conn_dense(k0, h)
        h = jax.nn.relu(h) * 2
        h = s1 * _conn_dense(k1, h)
        h = jax.nn.relu(h) * 2
        h = s2 * _conn_dense(k2, h)
        return h

    def _L3_xattn_ref(src, tgt, src_mask, tgt_mask, W_src, b_src, W_tgt, b_tgt, W_out, b_out):
        import jax, jax.numpy as jnp
        import numpy as np
        B, S, T = (32, 128, 128)
        SRC_SIZE, TGT_SIZE, OUT_SIZE, NUM_HEAD = (512, 256, 256, 8)
        HEAD_DIM = OUT_SIZE // NUM_HEAD
        b, s, _ = src.shape
        t = tgt.shape[1]
        src_trans = jnp.einsum('bsf,of->bso', src, W_src) + b_src
        tgt_trans = jnp.einsum('btf,of->bto', tgt, W_tgt) + b_tgt
        src_trans = src_trans * src_mask[:, :, None]
        tgt_trans = tgt_trans * tgt_mask[:, :, None]
        src_key, src_val = jnp.split(src_trans, 2, axis=2)
        k = src_key.reshape(b, s, NUM_HEAD, HEAD_DIM)
        v = src_val.reshape(b, s, NUM_HEAD, HEAD_DIM)
        q = tgt_trans.reshape(b, t, NUM_HEAD, HEAD_DIM)
        scores = jnp.einsum('bthd,bshd->bhts', q, k) / np.sqrt(HEAD_DIM)
        scores = jnp.where(src_mask[:, None, None, :] == 0, -jnp.inf, scores)
        attn = jax.nn.softmax(scores, axis=-1)
        tgt_update = jnp.einsum('bhts,bshd->bthd', attn, v).reshape(b, t, OUT_SIZE)
        cat_tgt = jnp.concatenate([tgt, tgt_update], axis=2)
        return jnp.einsum('btf,of->bto', cat_tgt, W_out) + b_out

    def _L3_ffn_ref(x, in_proj_w, in_proj_b, out_proj_w, out_proj_b, ln1_g, ln1_b, ln2_g, ln2_b, wg, w1, b1, w2, b2):
        import jax, jax.numpy as jnp
        import numpy as np
        D = 256
        H = 4
        HD = D // H
        E = 8
        FF = 1024
        CAP_FACTOR = 1.0

        def _ln(x, g, b, eps=1e-05):
            mu = jnp.mean(x, -1, keepdims=True)
            v = jnp.mean((x - mu) ** 2, -1, keepdims=True)
            return (x - mu) * jax.lax.rsqrt(v + eps) * g + b

        def _mha(x, w, b, ow, ob):
            L, N, _ = x.shape
            qkv = x @ w.T + b
            q, k, v = jnp.split(qkv, 3, axis=-1)
            rh = lambda t: t.reshape(L, N, H, HD).transpose(1, 2, 0, 3)
            q, k, v = (rh(q), rh(k), rh(v))
            scores = jnp.einsum('nhld,nhmd->nhlm', q, k) / np.float32(np.sqrt(HD))
            attn = jax.nn.softmax(scores, axis=-1)
            o = jnp.einsum('nhlm,nhmd->nhld', attn, v).transpose(2, 0, 1, 3).reshape(L, N, D)
            return o @ ow.T + ob

        def _moe(x, wg, w1, b1, w2, b2):
            L, N, _ = x.shape
            S = L * N
            cap = int(CAP_FACTOR * S) // E
            xf = x.reshape(S, D)
            gates = jax.nn.softmax(xf @ wg, axis=-1)
            idx = jnp.argmax(gates, axis=-1)
            mask1 = jax.nn.one_hot(idx, E, dtype=x.dtype)
            loc = jnp.sum((jnp.cumsum(mask1, 0) - 1.0) * mask1, -1).astype(jnp.int32)
            keep = loc < cap
            gate_val = jnp.take_along_axis(gates, idx[:, None], -1)[:, 0]
            slot = jnp.where(keep, idx.astype(jnp.int32) * cap + loc, E * cap)
            disp = jnp.zeros((E * cap, D), x.dtype).at[slot].set(xf, mode='drop')
            disp = disp.reshape(E, cap, D)
            h = jnp.einsum('ecd,edf->ecf', disp, w1) + b1[:, None, :]
            y = (jnp.einsum('ecf,efd->ecd', h, w2) + b2[:, None, :]).reshape(E * cap, D)
            out = jnp.where(keep[:, None], gate_val[:, None] * y[jnp.minimum(slot, E * cap - 1)], 0.0)
            return out.reshape(L, N, D)
        y1 = _ln(x + _mha(x, in_proj_w, in_proj_b, out_proj_w, out_proj_b), ln1_g, ln1_b)
        y2 = _ln(y1 + _moe(y1, wg, w1, b1, w2, b2), ln2_g, ln2_b)
        return y2
    x = x + _L0_xattn_ref(_layernorm(x, axis=-1), ctx_2048, mask_BxS2_if0, L0_xattn_W_in, L0_xattn_b_in, L0_xattn_g_res, L0_xattn_g_init)
    x = x + _L0_ffn_ref(_layernorm(x, axis=-1), L0_ffn_g_info, L0_ffn_W_qkv, L0_ffn_W_proj, L0_ffn_b_proj)
    x = x + _L1_xattn_ref(_layernorm(x, axis=-1), ctx_2048, L1_xattn_w_qkv, L1_xattn_w_proj, L1_xattn_b_proj)
    x = x + _L1_ffn_ref(_layernorm(x, axis=-1), L1_ffn_router_w, L1_ffn_w1, L1_ffn_w2)
    x = x + _L2_xattn_ref(_layernorm(x, axis=-1), ctx_2048, L2_xattn_Wq, L2_xattn_Wkv, L2_xattn_null_kv, L2_xattn_Wout, L2_xattn_ln_scale, L2_xattn_ln_bias)
    x = x + _L2_ffn_ref(_layernorm(x, axis=-1), L2_ffn_k0, L2_ffn_k1, L2_ffn_k2, L2_ffn_s0, L2_ffn_s1, L2_ffn_s2)
    x = x + _L3_xattn_ref(ctx_2048, _layernorm(x, axis=-1), mask_BxS2_fk1, mask_BxS2_fk1, L3_xattn_W_src, L3_xattn_b_src, L3_xattn_W_tgt, L3_xattn_b_tgt, L3_xattn_W_out, L3_xattn_b_out)
    x = x + _L3_ffn_ref(_layernorm(x, axis=-1), L3_ffn_in_proj_w, L3_ffn_in_proj_b, L3_ffn_out_proj_w, L3_ffn_out_proj_b, L3_ffn_ln1_g, L3_ffn_ln1_b, L3_ffn_ln2_g, L3_ffn_ln2_b, L3_ffn_wg, L3_ffn_w1, L3_ffn_b1, L3_ffn_w2, L3_ffn_b2)
    return x

_drawn_inputs = setup_inputs


def setup_inputs(seed=0):
    import zlib

    import numpy as np

    out = dict(_drawn_inputs(seed))
    spreads = {'L0_xattn_b_in': (0.0, 0.1),
     'L0_xattn_g_res': (1.0, 0.2),
     'L0_xattn_g_init': (1.0, 0.2),
     'L0_ffn_b_proj': (0.0, 0.1),
     'L2_xattn_ln_scale': (1.0, 0.2),
     'L2_xattn_ln_bias': (0.0, 0.1),
     'L3_xattn_b_src': (0.0, 0.311),
     'L3_xattn_b_tgt': (0.0, 0.8),
     'L3_xattn_b_out': (0.0, 0.1),
     'L3_ffn_in_proj_b': (0.0, 0.8),
     'L3_ffn_out_proj_b': (0.0, 0.1),
     'L3_ffn_ln1_g': (1.0, 0.2),
     'L3_ffn_ln1_b': (0.0, 0.305),
     'L3_ffn_ln2_g': (1.0, 0.2),
     'L3_ffn_ln2_b': (0.0, 0.311),
     'L3_ffn_b1': (0.0, 0.8),
     'L3_ffn_b2': (0.0, 2.0)}
    factors = {'L0_ffn_g_info': 23.64,
     'L1_xattn_w_qkv': 4.377,
     'L1_xattn_b_proj': 5.331,
     'L1_ffn_router_w': 3.511,
     'L1_ffn_w1': 3.33,
     'L1_ffn_w2': 3.035,
     'L2_xattn_null_kv': 8.0,
     'L3_ffn_in_proj_w': 3.362,
     'L3_ffn_out_proj_w': 3.042,
     'L3_ffn_wg': 6.758,
     'L3_ffn_w1': 6.649,
     'L3_ffn_w2': 6.501}
    for name, (base, spread) in spreads.items():
        noise = np.random.default_rng([zlib.crc32(name.encode()), seed]).standard_normal(out[name].shape)
        drawn = base * np.exp(spread * noise) if base else spread * noise
        out[name] = jnp.asarray(drawn.astype(out[name].dtype))
    for name, factor in factors.items():
        out[name] = (out[name] * factor).astype(out[name].dtype)
    return out
```

```python
from contextlib import ExitStack
import math

import numpy as np
import concourse.bass as bass
from concourse import mybir

STAGES = 8

F32 = mybir.dt.float32
BF16 = mybir.dt.bfloat16
I32 = mybir.dt.int32
U32 = mybir.dt.uint32
U8 = mybir.dt.uint8
ALU = mybir.AluOpType
ACT = mybir.ActivationFunctionType
AX = mybir.AxisListType
ds = bass.ds

B, N, D = 8, 256, 256
T = B * N
P = 128
KD = D // P
GT = 512
NG = T // GT
DC = 512
KC = DC // P
REG = 5
EPS = 1e-5
BIG = float(2.0 ** 100)
A_LOGP = 0.001
DT = -math.log(-math.expm1(-A_LOGP))


def shape_constants():
    p = np.arange(P)[:, None]
    f = np.arange(P)[None, :]
    parts = {}
    parts["ident"] = (p == f)
    parts["tri"] = (p < f)
    parts["mean"] = np.full((P, P), 1.0 / D)
    parts["ones"] = np.ones((P, P))
    parts["iota"] = np.broadcast_to(np.arange(N)[None, :], (P, N))
    parts["chan"] = np.concatenate([p, p + P, -p, -(p + P)], axis=1)
    hm = np.arange(16)[None, None, :] == (np.arange(2)[None, :, None] * 8 + p[:, :, None] // 16)
    parts["head16"] = hm.reshape(P, 32)
    parts["even16"] = np.concatenate([0.25 * ((p // 16) % 2 == 0), 0.25 * ((p // 16) % 2 == 1)], axis=1)
    parts["half5"] = np.where(p < REG, 0.5, 1.0)
    parts["regblk"] = (p // REG == np.arange(D)[None, :] // 16)
    parts["regsum"] = 0.5 * ((p % REG == np.arange(REG)[None, :]) & (p < 16 * REG))
    n16 = (f % 16)
    parts["posq"] = np.where(p < 16, n16 == p, 0)
    parts["posk"] = np.where(p < 16, -BIG * (n16 != p), 0)
    parts["iota8"] = np.broadcast_to(np.arange(8)[None, :], (P, 8))
    parts["token"] = (np.arange(16)[None, :] * P + p) + T
    at, cols = {}, 0
    for k, v in parts.items():
        at[k] = (cols, v.shape[1])
        cols += v.shape[1]
    return at, np.concatenate([v.astype(np.float32) for v in parts.values()], axis=1)


CONST_AT, _ = shape_constants()
CONST_COLS = sum(n for _, n in CONST_AT.values())


class Program:
    pass


def feature_rows(w):
    return w.rearrange("(k p) m -> p k m", p=P)


def build(nc, A, out):
    top = ExitStack()
    with top:
        g = Program()
        g.nc, g.A = nc, A

        def sb(name, shape, dt=F32, ctx=top):
            return ctx.enter_context(nc.sbuf_tensor(name, shape, dt))

        g.used = []

        def sem(name):
            s = nc.alloc_semaphore(name=name)
            g.used.append(s)
            return s

        def end_layer():
            nc.clear_and_free_semaphores(g.used)
            nc.all_engine_barrier()
            g.used = []

        g.sb, g.sem = sb, sem
        g.bank = [top.enter_context(nc.psum_tensor(f"bank{i}", [P, 512], F32)) for i in range(8)]
        g.X = sb("X", [P, KD, T])
        g.XN = sb("XN", [P, KD, T])
        g.cst = sb("cst", [P, CONST_COLS])
        g.c = lambda name: g.cst[:, CONST_AT[name][0]:CONST_AT[name][0] + CONST_AT[name][1]]
        g.eps5 = sb("eps5", [P, 1])
        g.eps6 = sb("eps6", [P, 1])
        g.ln_cent = sb("ln_cent", [P, 2, KD, GT])
        g.ln_sq = sb("ln_sq", [P, 2, KD, GT])
        g.ln_std = sb("ln_std", [P, 2, 4])
        g.ln_rstd = sb("ln_rstd", [P, 2, 4])
        g.ln_rm = sb("ln_rm", [P, 2, 3, 4])
        g.hold = sb("hold", [P, 1])
        g.pool_hold = sb("pool_hold", [P, 1])
        g.onesb = sb("onesb", [P, P], BF16)
        start_phase(g)
        if STAGES >= 1:
            depool_layer(g)
            end_layer()
        if STAGES >= 2:
            layer_norm_phase(g, "n0f")
            register_attention_layer(g)
            end_layer()
        if STAGES >= 3:
            layer_norm_phase(g, "n1x")
            context_attention_layer(g)
            end_layer()
        if STAGES >= 4:
            layer_norm_phase(g, "n1f")
            routed_ffn_layer(g)
            end_layer()
        if STAGES >= 5:
            layer_norm_phase(g, "n2x")
            null_attention_layer(g)
            end_layer()
        if STAGES >= 6:
            layer_norm_phase(g, "n2f")
            sign_ffn_layer(g)
            end_layer()
        if STAGES >= 7:
            layer_norm_phase(g, "n3x")
            masked_attention_layer(g)
            end_layer()
        if STAGES >= 8:
            layer_norm_phase(g, "n3f")
            position_attention_layer(g)
            end_layer()
            expert_layer(g)
            end_layer()
        store_phase(g, out)


def hold_pool(g, po):
    return po.tensor_tensor(g.pool_hold[:], g.eps5[:], g.eps6[:], ALU.add)


def start_phase(g):
    nc = g.nc
    loaded = g.sem("start_loaded")
    g.made = made = nc.alloc_semaphore(name="start_made")
    with nc.Block() as block:
        @block.sync
        def _(sp):
            sp.dma_start(g.cst[:], g.A["const"]).then_inc(loaded, 16)
            sp.dma_start(g.X[:], feature_rows(g.A["x"])).then_inc(loaded, 16)
            sp.wait_ge(loaded, 32)

        @block.vector
        def _(v):
            v.memset(g.eps5[:], EPS).then_inc(made, 1)
            v.memset(g.eps6[:], 1e-6).then_inc(made, 1)
            v.memset(g.onesb[:], 1.0).then_inc(made, 1)


def store_phase(g, out):
    nc = g.nc
    stored = g.sem("stored")
    with nc.Block() as block:
        @block.sync
        def _(sp):
            sp.dma_start(feature_rows(out), g.X[:]).then_inc(stored, 16)
            sp.wait_ge(stored, 16)



def layer_norm_phase(g, tag, src=None, dst=None, gain=None, shift=None, resid=None, rms_gain=None, eps=None):
    nc = g.nc
    src = g.X if src is None else src
    dst = g.XN if dst is None else dst
    eps = g.eps5 if eps is None else eps
    ident, mean = g.c("ident"), g.c("mean")
    names = ["mean_ready", "centred", "squared", "var_ready", "std_ready", "rstd_ready", "spread", "normed"]
    S = Program()
    (S.mean_ready, S.centred, S.squared, S.var_ready, S.std_ready, S.rstd_ready, S.spread, S.normed) = (
        g.sem(f"{tag}_{n}") for n in names)
    rm = g.sem(f"{tag}_rms_step")
    rmstd = g.sem(f"{tag}_rms_std")
    written = g.sem(f"{tag}_written")
    with nc.Block() as block:
        @block.tensor
        def _(pe):
            with pe.Fori(0, NG // 2) as pair:
                gi = 2 * pair
                for j in range(2):
                    for k in range(KD):
                        mm = pe.matmul(g.bank[j][:], mean, src[:, k, ds((gi + j) * GT, GT)],
                                       start=(k == 0), stop=(k == KD - 1))
                    mm.then_inc(S.mean_ready, 1)
                for j in range(2):
                    pe.wait_ge(S.squared, gi + j + 1)
                    for t in range(4):
                        for k in range(KD):
                            mm = pe.matmul(g.bank[2 + j][:, t:t + 1], g.ln_sq[:, j, k, t * P:(t + 1) * P],
                                           mean[:, 0:1], start=(k == 0), stop=(k == KD - 1))
                    mm.then_inc(S.var_ready, 1)
                for j in range(2):
                    pe.wait_ge(S.rstd_ready, gi + j + 1)
                    for t in range(4):
                        mm = pe.matmul(g.bank[4 + j][:, t * P:(t + 1) * P],
                                       g.ln_rstd[:, j, t:t + 1].to_broadcast([P, P]), ident, start=True, stop=True)
                    mm.then_inc(S.spread, 1)

        @block.scalar
        def _(act):
            with act.Fori(0, NG // 2) as pair:
                gi = 2 * pair
                for j in range(2):
                    act.wait_ge(S.centred, gi + j + 1)
                    act.activation(g.ln_sq[:, j], g.ln_cent[:, j], ACT.Square).then_inc(S.squared, 1)
                for j in range(2):
                    act.wait_ge(S.var_ready, gi + j + 1)
                    act.activation(g.ln_std[:, j], g.bank[2 + j][:, 0:4], ACT.Sqrt, bias=eps[:])\
                       .then_inc(S.std_ready, 1)
                    if rms_gain is not None:
                        act.wait_ge(rm, 2 * (gi + j) + 2)
                        act.activation(g.ln_rm[:, j, 1], g.ln_rm[:, j, 0], ACT.Sqrt, bias=g.eps5[:])\
                           .then_inc(rmstd, 1)

        @block.vector
        def _(v):
            with v.Fori(0, NG // 2) as pair:
                gi = 2 * pair
                for j in range(2):
                    v.wait_ge(S.mean_ready, gi + j + 1)
                    v.tensor_tensor(g.ln_cent[:, j], src[:, :, ds((gi + j) * GT, GT)],
                                    g.bank[j][:].unsqueeze(1).to_broadcast([P, KD, GT]), ALU.subtract)\
                     .then_inc(S.centred, 1)
                for j in range(2):
                    v.wait_ge(S.std_ready, gi + j + 1)
                    if rms_gain is None:
                        v.reciprocal(g.ln_rstd[:, j], g.ln_std[:, j]).then_inc(S.rstd_ready, 1)
                    else:
                        v.reciprocal(g.ln_std[:, j], g.ln_std[:, j]).then_inc(rm, 1)
                        v.wait_ge(rm, 2 * (gi + j) + 1)
                        v.tensor_tensor(g.ln_rm[:, j, 2], g.bank[2 + j][:, 0:4], g.ln_std[:, j], ALU.mult)\
                         .then_inc(S.normed, 1)
                        v.wait_ge(S.normed, 3 * (gi + j) + 1)
                        v.tensor_tensor(g.ln_rm[:, j, 0], g.ln_rm[:, j, 2], g.ln_std[:, j], ALU.mult).then_inc(rm, 1)
                        v.wait_ge(rmstd, gi + j + 1)
                        v.reciprocal(g.ln_rm[:, j, 1], g.ln_rm[:, j, 1]).then_inc(S.normed, 1)
                        v.wait_ge(S.normed, 3 * (gi + j) + 2)
                        v.tensor_tensor(g.ln_rstd[:, j], g.ln_rm[:, j, 1], g.ln_std[:, j], ALU.mult)\
                         .then_inc(S.rstd_ready, 1)
                        v.nop().then_inc(S.normed, 1)
                for j in range(2):
                    v.wait_ge(S.spread, gi + j + 1)
                    for k in range(KD):
                        o = dst[:, k, ds((gi + j) * GT, GT)]
                        if rms_gain is not None:
                            w = v.scalar_tensor_tensor(o, g.ln_cent[:, j, k], rms_gain[:, k:k + 1],
                                                       g.bank[4 + j][:], ALU.mult, ALU.mult)
                        elif gain is None:
                            w = v.tensor_tensor(o, g.ln_cent[:, j, k], g.bank[4 + j][:], ALU.mult)
                        else:
                            done = v.scalar_tensor_tensor(g.ln_sq[:, j, k], g.ln_cent[:, j, k], gain[:, k:k + 1],
                                                          g.bank[4 + j][:], ALU.mult, ALU.mult)
                            done.then_inc(S.normed, 1)
                            v.wait_ge(S.normed, KD * (gi + j) + k + 1)
                            if resid is None:
                                w = v.tensor_scalar(o, g.ln_sq[:, j, k], shift[:, k:k + 1], None, ALU.add)
                            else:
                                w = v.scalar_tensor_tensor(o, g.ln_sq[:, j, k], shift[:, k:k + 1],
                                                           resid[:, k, ds((gi + j) * GT, GT)], ALU.add, ALU.add)
                        w.then_inc(written, 1)
                v.wait_ge(written, KD * (gi + 2))



def depool_layer(g):
    nc, A = g.nc, g.A
    ident, iota, chan = g.c("ident"), g.c("iota"), g.c("chan")
    with ExitStack() as ctx:
        sb = lambda n, s, dt=F32: g.sb("dp_" + n, s, dt, ctx)
        W = sb("W", [P, KD, D])
        bias = sb("bias", [P, KD])
        gres = sb("gres", [P, KD])
        ginit = sb("ginit", [P, D])
        lens = sb("lens", [B, N], I32)
        lensf = sb("lensf", [B, N])
        zeros = sb("zeros", [P, N])
        ends = sb("ends", [B, N])
        wrap = sb("wrap", [B, N])
        endsT = sb("endsT", [P, 2, B])
        col = sb("col", [P, 2])
        hit = sb("hit", [P, 2, N], BF16)
        bnd = sb("bnd", [P, N])
        count = sb("count", [P, N])
        plug = sb("plug", [P, T])
        loaded, s1, tr, ct, cp = (g.sem("dp_" + n) for n in ("loaded", "step", "turned", "hits", "plugs"))
        with nc.Block() as block:
            @block.sync
            def _(sp):
                sp.dma_start(lens[:], A["mask_BxS2_if0"]).then_inc(loaded, 16)
                sp.dma_start(W[:], feature_rows(A["L0_xattn_W_in"])).then_inc(loaded, 16)
                sp.dma_start(bias[:], A["L0_xattn_b_in_col"]).then_inc(loaded, 16)
                sp.dma_start(gres[:], A["L0_xattn_g_res_col"]).then_inc(loaded, 16)
                sp.dma_start(ginit[:], A["L0_xattn_g_init"][0:D].unsqueeze(0).to_broadcast([P, D])).then_inc(loaded, 16)
                sp.wait_ge(loaded, 80)

            @block.tensor
            def _(pe):
                pe.wait_ge(s1, 6)
                for c in range(2):
                    mm = pe.transpose(g.bank[0][:, c * B:(c + 1) * B], ends[:, c * P:(c + 1) * P], ident[0:B, 0:B])
                mm.then_inc(tr, 1)
                with pe.Fori(0, B) as b:
                    pe.wait_ge(ct, 2 * b + 2)
                    for c in range(2):
                        mm = pe.matmul(g.bank[1][:, 0:N], g.onesb[:], hit[:, c], start=(c == 0), stop=(c == 1))
                    mm.then_inc(tr, 1)

            @block.vector
            def _(v):
                v.wait_ge(loaded, 80)
                v.memset(zeros[:], 0.0).then_inc(s1, 1)
                v.tensor_scalar(lensf[:], lens[:], float(N + 1), None, ALU.min).then_inc(s1, 1)
                v.wait_ge(s1, 2)
                v.tensor_tensor_scan(ends[:], lensf[:], zeros[0:B], 0.0, ALU.add, ALU.add).then_inc(s1, 1)
                v.wait_ge(s1, 3)
                v.tensor_scalar(ends[:], ends[:], -1.0, None, ALU.add).then_inc(s1, 1)
                v.wait_ge(s1, 4)
                v.tensor_scalar(wrap[:], ends[:], 0.0, float(N), ALU.is_lt, ALU.mult).then_inc(s1, 1)
                v.wait_ge(s1, 5)
                v.tensor_tensor(ends[:], ends[:], wrap[:], ALU.add).then_inc(s1, 1)
                v.wait_ge(tr, 1)
                v.tensor_copy(endsT[:].rearrange("p a b -> p (a b)"), g.bank[0][:, 0:2 * B]).then_inc(s1, 1)
                v.wait_ge(s1, 7)
                with v.Fori(0, B) as b:
                    v.tensor_copy(col[:].unsqueeze(2), endsT[:, :, ds(b, 1)]).then_inc(cp, 1)
                    v.wait_ge(cp, 4 * b + 1)
                    for c in range(2):
                        v.tensor_scalar(hit[:, c], iota, col[:, c:c + 1], None, ALU.is_equal).then_inc(ct, 1)
                    v.wait_ge(tr, b + 2)
                    v.tensor_scalar(bnd[:], g.bank[1][:, 0:N], 1.0, None, ALU.min).then_inc(cp, 1)
                    v.wait_ge(cp, 4 * b + 2)
                    v.tensor_tensor_scan(count[:], bnd[:], zeros[:], 0.0, ALU.add, ALU.add).then_inc(cp, 1)
                    v.wait_ge(cp, 4 * b + 3)
                    v.tensor_scalar(plug[:, ds(b * N, N)], count[:], -1.0, 0.0, ALU.add, ALU.max).then_inc(cp, 1)
                    v.wait_ge(cp, 4 * b + 4)

        layer_norm_phase(g, "n0x", rms_gain=gres)

        cx = sb("cx", [P, 2, 4, DC])
        sq = sb("sq", [P, DC])
        ss = sb("ss", [P, 4])
        rs = sb("rs", [P, 4])
        u = sb("u", [P, 4, D])
        age = sb("age", [P, 2, GT])
        live = sb("live", [P, 2, GT])
        gd = sb("gd", [P, 2, GT])
        ld = [g.sem(f"dq_loaded{j}") for j in range(2)]
        aged, dec, sums, std, rec, us, mm2, done = (g.sem("dq_" + n) for n in (
            "aged", "decayed", "sums", "std", "rec", "patches", "out_ready", "group_done"))
        with nc.Block() as block:
            @block.sync
            def _(sp):
                def load(gi, j):
                    sp.dma_start(cx[:, j], A["ctx_tok"][ds(gi * GT, GT), :].rearrange("(t p) d -> p t d", p=P))\
                      .then_inc(ld[j], 16)
                load(0, 0)
                load(1, 1)
                with sp.Fori(0, NG // 2 - 1) as pair:
                    gi = 2 * pair
                    for j in range(2):
                        sp.wait_ge(done, gi + j + 1)
                        load(gi + j + 2, j)

            @block.scalar
            def _(act):
                with act.Fori(0, NG // 2) as pair:
                    g0 = 2 * pair
                    for j in range(2):
                        gi = g0 + j
                        act.wait_ge(ld[j], 16 * pair + 16)
                        for t in range(4):
                            act.activation(sq[:], cx[:, j, t], ACT.Square, accum_out=ss[:, t:t + 1]).then_inc(sums, 1)
                            act.wait_ge(sums, 4 * gi + t + 1)
                        act.activation(rs[:], ss[:], ACT.Sqrt, scale=1.0 / DC, bias=g.eps5[:]).then_inc(std, 1)
                        act.wait_ge(aged, 4 * gi + 4)
                        act.activation(gd[:], age[:], ACT.Exp, scale=-DT, bias=0.0).then_inc(dec, 1)
                        act.wait_ge(done, gi + 1)

            @block.vector
            def _(v):
                with v.Fori(0, NG // 2) as pair:
                    g0 = 2 * pair
                    for j in range(2):
                        gi = g0 + j
                        pl = plug[:, ds(gi * GT, GT)]
                        for c in range(2):
                            v.tensor_scalar(age[:, c], pl, chan[:, 2 + c:3 + c], 0.0, ALU.add, ALU.max).then_inc(aged, 1)
                            v.tensor_scalar(live[:, c], pl, chan[:, c:c + 1], math.exp(-A_LOGP), ALU.is_ge, ALU.mult)\
                             .then_inc(aged, 1)
                        v.wait_ge(std, gi + 1)
                        v.reciprocal(rs[:], rs[:]).then_inc(rec, 1)
                        v.wait_ge(rec, gi + 1)
                        for t in range(4):
                            v.scalar_tensor_tensor(u[:, t], cx[:, j, t, 0:D], rs[:, t:t + 1], ginit[:],
                                                   ALU.mult, ALU.mult).then_inc(us, 1)
                        v.wait_ge(dec, gi + 1)
                        v.wait_ge(aged, 4 * gi + 4)
                        v.tensor_tensor(gd[:], gd[:], live[:], ALU.mult).then_inc(us, 1)
                        v.wait_ge(mm2, gi + 1)
                        for m in range(KD):
                            xo = g.X[:, m, ds(gi * GT, GT)]
                            o = v.scalar_tensor_tensor(xo, g.bank[m][:], bias[:, m:m + 1], xo, ALU.add, ALU.add)
                        o.then_inc(done, 1)
                        v.wait_ge(done, gi + 1)

            @block.tensor
            def _(pe):
                with pe.Fori(0, NG) as gi:
                    pe.wait_ge(us, 5 * gi + 5)
                    for m in range(KD):
                        for k in range(KD):
                            pe.matmul(g.bank[m][:], W[:, k, m * P:(m + 1) * P], g.XN[:, k, ds(gi * GT, GT)],
                                      start=(k == 0), stop=False, skip_group_check=True)
                        for bb in range(2):
                            for c in range(2):
                                mm = pe.matmul(g.bank[m][:, bb * N:(bb + 1) * N], u[:, 2 * bb + c, m * P:(m + 1) * P],
                                               gd[:, c, bb * N:(bb + 1) * N], start=False,
                                               stop=(c == 1 and bb == 1), skip_group_check=True)
                    mm.then_inc(mm2, 1)
                    pe.wait_ge(done, gi + 1)



def attention_block(g, ctx, tag, heads, dh, per_unit, keys, load, front, q_of, k_of, v_of, wout, finish,
                    mask=None, gather=None, null=None, reg=None, weights=None, n_weights=0, n_loads=0,
                    n_gather=0, wide_gather=False, units=None):
    nc = g.nc
    ident = g.c("ident")
    W = per_unit * keys
    UT = heads // per_unit
    if units is None:
        units = [[t * per_unit + hh for hh in range(per_unit)] for t in range(UT)]
    KCH = [(c * P, min(P, keys - c * P)) for c in range(keys // P)]
    U = 2 * UT
    OC = heads * dh // P
    OB = max(1, heads * dh // 512)
    RND = max(1, OC // 4)
    sb = lambda n, s, dt=F32: g.sb(f"{tag}_{n}", s, dt, ctx)
    xb = sb("xb", [P, KD, N])
    nmax = sb("nmax", [P, 4, per_unit])
    prob = sb("prob", [P, 4, W])
    probT = sb("probT", [P, 3, 512])
    sums = sb("sums", [P, 2, heads])
    inv = sb("inv", [P, 2, heads])
    outn = sb("outn", [P, 2, heads * dh])
    outT = sb("outT", [P, OC, N])
    if null is not None:
        pnull = sb("pnull", [P, 2, heads])
        pnullT = sb("pnullT", [heads, P])
    if reg is not None:
        rq0 = sb("rq0", [P, KD, REG])
        rq = sb("rq", [P, KD, 16, REG])
        rp = sb("rp", [16 * REG, N])
        rpT = sb("rpT", [P, 2, 16 * REG])
        rst = sb("rst", [16 * REG, 4])
        ro = sb("ro", [16 * REG, N])
        rout = sb("rout", [REG, N])
    wl = g.sem(tag + "_weights")
    ld = [g.sem(f"{tag}_loaded{j}") for j in range(2)]
    (xc, fp, fv, fa, qk, mx, ex, tp, pt, pv, sm, nrm, ott, otc, pr, bd, rgp, rgv, rga) = (g.sem(f"{tag}_{n}") for n in (
        "batch_copied", "front_product", "front_by_vector", "front_by_scalar", "scores", "maxima", "exps",
        "turned", "turned_copied", "values", "sums_step", "divided", "out_turned", "out_copied", "projected",
        "batch_done", "reg_product", "reg_vector", "reg_exp"))
    NFV = sum(1 for f in front if f[0] == "v")
    NFA = sum(1 for f in front if f[0] == "a")
    S = [g.bank[i] for i in range(3)]
    PT = [g.bank[3], g.bank[4]]
    O = lambda i: ([g.bank[5 + i]] if OB == 1 else [g.bank[5], g.bank[6]])
    M = g.bank[7]
    NORMS = 2 if reg is None else 3
    smn = {"n": 0}

    with nc.Block() as block:
        @block.sync
        def _(sp):
            for w in weights(sp):
                w.then_inc(wl, 16)
            if n_loads == 0:
                sp.wait_ge(wl, 16 * n_weights)
                return
            for j in range(2):
                for d in load(sp, j, j):
                    d.then_inc(ld[j], 16)
            with sp.Fori(0, B // 2 - 1) as pair:
                for j in range(2):
                    sp.wait_ge(bd, 2 * pair + j + 1)
                    for d in load(sp, 2 * pair + j + 2, j):
                        d.then_inc(ld[j], 16)
            sp.wait_ge(wl, 16 * n_weights)

        @block.gpsimd
        def _(po):
            with po.Fori(0, B) as b:
                if gather is None:
                    po.tensor_copy(xb[:], g.XN[:, :, ds(b * N, N)]).then_inc(xc, 1)
                else:
                    for n, c in enumerate(gather(po, b, xb)):
                        c.then_inc(xc, 1)
                        po.wait_ge(xc, n_gather * b + n + 1)
                        if n + 1 < n_gather and wide_gather:
                            hold_pool(g, po)
                po.wait_ge(bd, b + 1)
        NXC = 1 if gather is None else n_gather

        @block.tensor
        def _(pe):
            pe.wait_ge(wl, 16 * n_weights)
            with pe.Fori(0, B // 2) as pair:
                for j in range(2):
                    b = 2 * pair + j
                    pe.wait_ge(xc, NXC * b + NXC)
                    if n_loads:
                        pe.wait_ge(ld[j], 16 * n_loads * pair + 16 * n_loads)
                    for n, (who, product, _) in enumerate(front):
                        if n >= 4:
                            before = sum(1 for f in front[:n - 4 + 1] if f[0] == front[n - 4][0])
                            if front[n - 4][0] == "v":
                                pe.wait_ge(fv, NFV * b + before)
                            else:
                                pe.wait_ge(fa, NFA * b + before)
                        product(pe, g.bank[n % 4], j, b, xb).then_inc(fp, 1)
                    if NFV:
                        pe.wait_ge(fv, NFV * b + NFV)
                    if NFA:
                        pe.wait_ge(fa, NFA * b + NFA)
                    if reg is not None:
                        pe.wait_ge(rgv, 8 * b + 3)
                        R, RN = g.bank[6], 16 * REG
                        pe.matmul(R[0:RN, 0:N], reg["q_mask"], reg["k_mask"](b), start=True, stop=False)
                        for k in range(KD):
                            mm = pe.matmul(R[0:RN, 0:N], rq[:, k].rearrange("p h r -> p (h r)"), reg["k"](k),
                                           start=False, stop=(k == KD - 1))
                        mm.then_inc(rgp, 1)
                        pe.wait_ge(rga, b + 1)
                        for c in range(2):
                            mm = pe.transpose(M[:, c * RN:(c + 1) * RN], rp[:, c * P:(c + 1) * P], ident[0:RN, 0:RN])
                        mm.then_inc(rgp, 1)
                        pe.wait_ge(rgv, 8 * b + 5)
                        for c in range(2):
                            mm = pe.matmul(R[0:RN, 0:N], rpT[:, c], reg["v"](c), start=(c == 0), stop=(c == 1))
                        mm.then_inc(rgp, 1)
                        pe.wait_ge(rgv, 8 * b + 7)
                        pe.matmul(M[0:REG, 256:512], g.c("regsum")[0:RN, :], ro[:], start=True, stop=True)\
                          .then_inc(rgp, 1)
                        pe.wait_ge(rgv, 8 * b + 8)

                    def scores(u):
                        i, hs = u // UT, units[u % UT]
                        s = S[u % 3]
                        if mask is not None:
                            ml, mr = mask(i, b, hs)
                            pe.matmul(s[:, 0:W], ml, mr, start=True, stop=False, skip_group_check=True)
                        for hh, h in enumerate(hs):
                            mm = pe.matmul(s[:, hh * keys:(hh + 1) * keys], q_of(h, i, j), k_of(h, i, j),
                                           start=(mask is None), stop=(hh == per_unit - 1), skip_group_check=True)
                        mm.then_inc(qk, 1)

                    def turn(u):
                        pe.wait_ge(ex, U * b + u + 1)
                        n = 0
                        for hh in range(per_unit):
                            for c0, _ in KCH:
                                mm = pe.transpose(PT[u % 2][:, n * P:(n + 1) * P],
                                                  prob[:, u % 4, hh * keys + c0:hh * keys + c0 + P], ident)
                                n += 1
                        mm.then_inc(tp, 1)

                    def values(u):
                        i, hs = u // UT, units[u % UT]
                        pe.wait_ge(pt, U * b + u + 1)
                        if OB == 2 and u == UT:
                            pe.wait_ge(nrm, NORMS * b + 1)
                        n = 0
                        for h in hs:
                            col = h * dh
                            ob = O(i)[col // 512]
                            for c in range(len(KCH)):
                                mm = pe.matmul(ob[:, col % 512:col % 512 + dh], probT[:, u % 3, n * P:(n + 1) * P],
                                               v_of(h, c, i, j), start=(col % 512 == 0 and c == 0),
                                               stop=(c == len(KCH) - 1), skip_group_check=True)
                                n += 1
                        mm.then_inc(pv, 1)
                        if u % UT == UT - 1 and null is not None:
                            pe.wait_ge(pt, U * b + u + 1)
                            pe.transpose(M[0:heads, 0:P], pnull[:, i], ident).then_inc(ott, 1)
                            pe.wait_ge(otc, (2 * RND + 2) * b + (RND + 1) * i + 1)
                            for half in range(OB):
                                mm = pe.matmul(O(i)[half][:, :], pnullT[:], null[:, half * 512:(half + 1) * 512],
                                               start=False, stop=True, skip_group_check=True)
                            mm.then_inc(pv, 1)

                    def out_turn(i):
                        nrd = NORMS * b + (i + 1 if reg is None else (2 if i == 0 else 3))
                        pe.wait_ge(nrm, nrd)
                        extra = 1 if null is not None else 0
                        for r in range(RND):
                            if r:
                                pe.wait_ge(otc, (RND + extra) * (2 * b + i) + extra + r)
                            for c in range(OC // RND):
                                mm = pe.transpose(M[:, c * P:(c + 1) * P],
                                                  outn[:, i, (r * 4 + c) * P:(r * 4 + c + 1) * P], ident)
                            mm.then_inc(ott, 1)
                        pe.wait_ge(otc, (RND + extra) * (2 * b + i + 1))

                    for s in range(U + 3):
                        if s < U:
                            scores(s)
                        if s >= 2 and s - 2 < U:
                            turn(s - 2)
                        if s >= 3:
                            values(s - 3)
                        if s == UT + 4 and UT + 4 < U + 3:
                            out_turn(0)
                    if UT + 4 >= U + 3:
                        out_turn(0)
                    out_turn(1)
                    wout(pe, M, outT, xb).then_inc(pr, 1)
                    pe.wait_ge(bd, b + 1)

        @block.scalar
        def _(act):
            act.wait_ge(wl, 16 * n_weights)
            with act.Fori(0, B // 2) as pair:
                for j in range(2):
                    b = 2 * pair + j
                    for n, (who, _, evac) in enumerate(front):
                        if who == "a":
                            act.wait_ge(fp, len(front) * b + n + 1)
                            evac(act, g.bank[n % 4], j, b).then_inc(fa, 1)
                    if reg is not None:
                        act.wait_ge(rgv, 8 * b + 4)
                        act.activation(rp[:], g.bank[6][0:16 * REG, 0:N], ACT.Exp, bias=rst[:, 0:1],
                                       accum_out=rst[:, 1:2]).then_inc(rga, 1)
                    for u in range(U):
                        i, hs = u // UT, units[u % UT]
                        act.wait_ge(mx, U * b + u + 1)
                        if u >= 4:
                            act.wait_ge(pt, U * b + u - 3)
                        for hh in range(per_unit):
                            e = act.activation(prob[:, u % 4, hh * keys:(hh + 1) * keys],
                                               S[u % 3][:, hh * keys:(hh + 1) * keys], ACT.Exp,
                                               bias=nmax[:, u % 4, hh:hh + 1], accum_out=sums[:, i, hs[hh]:hs[hh] + 1])
                        e.then_inc(ex, 1)
                    act.wait_ge(bd, b + 1)

        @block.vector
        def _(v):
            v.wait_ge(wl, 16 * n_weights)
            with v.Fori(0, B // 2) as pair:
                for j in range(2):
                    b = 2 * pair + j
                    if n_loads:
                        v.wait_ge(ld[j], 16 * n_loads * pair + 16 * n_loads)
                    for n, (who, _, evac) in enumerate(front):
                        if who == "v":
                            v.wait_ge(fp, len(front) * b + n + 1)
                            evac(v, g.bank[n % 4], j, b).then_inc(fv, 1)
                    if reg is not None:
                        R, RN = g.bank[6], 16 * REG
                        v.wait_ge(fv, NFV * b + NFV)
                        v.tensor_tensor(rq0[:], reg["q"](0), reg["q"](1), ALU.add).then_inc(rgv, 1)
                        v.wait_ge(rgv, 8 * b + 1)
                        for k in range(KD):
                            v.tensor_tensor(rq[:, k], rq0[:, k].unsqueeze(1).to_broadcast([P, 16, REG]),
                                            g.c("head16")[:, 16 * k:16 * k + 16].unsqueeze(2)
                                            .to_broadcast([P, 16, REG]), ALU.mult).then_inc(rgv, 1)
                        v.wait_ge(rgp, 4 * b + 1)
                        v.tensor_reduce(rst[:, 0:1], R[0:RN, 0:N], AX.X, ALU.max, negate=True).then_inc(rgv, 1)
                        v.wait_ge(rgp, 4 * b + 2)
                        v.tensor_copy(rpT[:].rearrange("p c n -> p (c n)"), M[:, 0:2 * RN]).then_inc(rgv, 1)
                        v.wait_ge(rga, b + 1)
                        v.reciprocal(rst[:, 2:3], rst[:, 1:2]).then_inc(rgv, 1)
                        v.wait_ge(rgv, 8 * b + 6)
                        v.wait_ge(rgp, 4 * b + 3)
                        v.scalar_tensor_tensor(ro[:], R[0:RN, 0:N], rst[:, 2:3], g.c("regblk")[0:RN, :],
                                               ALU.mult, ALU.mult).then_inc(rgv, 1)
                        v.wait_ge(rgp, 4 * b + 4)
                        v.tensor_copy(rout[:], M[0:REG, 256:512]).then_inc(rgv, 1)

                    def take_null(i):
                        v.wait_ge(ott, (RND + 1) * (2 * b + i) + 1)
                        v.tensor_copy(pnullT[:], M[0:heads, 0:P]).then_inc(otc, 1)

                    def divide(i):
                        extra = 1 if null is not None else 0
                        v.wait_ge(ex, U * b + UT * (i + 1))
                        nst = 2 if (reg is not None) else 1
                        smb = (nst + 1 if reg is not None else 2) * b
                        v.reciprocal(inv[:, i], sums[:, i]).then_inc(sm, 1)
                        base = smb + i * (2 if reg is not None else 1)
                        v.wait_ge(sm, base + 1)
                        if reg is not None and i == 0:
                            v.tensor_scalar(inv[:, 0], inv[:, 0], g.c("half5"), None, ALU.mult).then_inc(sm, 1)
                            v.wait_ge(sm, base + 2)
                        v.wait_ge(pv, (U + 2 * extra) * b + UT * (i + 1) + extra * (i + 1))
                        for half in range(OB):
                            hs = heads // OB
                            d = v.tensor_tensor(
                                outn[:, i, half * hs * dh:(half + 1) * hs * dh].rearrange("p (h d) -> p h d", h=hs),
                                O(i)[half][:, 0:hs * dh].rearrange("p (h d) -> p h d", h=hs),
                                inv[:, i, half * hs:(half + 1) * hs].unsqueeze(2).to_broadcast([P, hs, dh]), ALU.mult)
                        d.then_inc(nrm, 1)
                        if reg is not None and i == 0:
                            v.wait_ge(nrm, NORMS * b + 1)
                            v.tensor_tensor(outn[0:REG, 0], outn[0:REG, 0], rout[:], ALU.add).then_inc(nrm, 1)

                    def out_copy(i):
                        extra = 1 if null is not None else 0
                        for r in range(RND):
                            v.wait_ge(ott, (RND + extra) * (2 * b + i) + extra + r + 1)
                            n = OC // RND
                            v.tensor_copy(outT[:, r * 4:r * 4 + n, i * P:(i + 1) * P],
                                          M[:, 0:n * P].rearrange("p (c q) -> p c q", c=n)).then_inc(otc, 1)

                    for s in range(U + 3):
                        if s < U:
                            v.wait_ge(qk, U * b + s + 1)
                            v.tensor_reduce(nmax[:, s % 4], S[s % 3][:, 0:W].rearrange("p (h k) -> p h k", h=per_unit),
                                            AX.X, ALU.max, negate=True).then_inc(mx, 1)
                        if s >= 2 and s - 2 < U:
                            u = s - 2
                            v.wait_ge(tp, U * b + u + 1)
                            if u >= 3:
                                v.wait_ge(pv, (U + 2 * (null is not None)) * b + u - 2 +
                                          (1 if null is not None and u - 3 >= UT else 0))
                            if null is not None:
                                v.tensor_copy(pnull[:, u // UT, u % UT:u % UT + 1], prob[:, u % 4, keys - 1:keys])
                            v.tensor_copy(probT[:, u % 3], PT[u % 2][:]).then_inc(pt, 1)
                        if s == UT + 2:
                            if null is not None:
                                take_null(0)
                            divide(0)
                        if s == UT + 4 and UT + 4 < U + 3:
                            out_copy(0)
                    if UT + 4 >= U + 3:
                        out_copy(0)
                    if null is not None:
                        take_null(1)
                    divide(1)
                    out_copy(1)
                    v.wait_ge(pr, b + 1)
                    f = finish(v, M, xb, b)
                    f.then_inc(bd, 1)
                    v.wait_ge(bd, b + 1)



def register_attention_layer(g):
    nc, A = g.nc, g.A
    with ExitStack() as ctx:
        sb = lambda n, s, dt=F32: g.sb("ra_" + n, s, dt, ctx)
        Wqkv = sb("Wqkv", [P, KD, 3 * D])
        qm = sb("qm", [P, T], BF16)
        km = sb("km", [P, B, 2, N], BF16)
        with ExitStack() as inner:
            ib = lambda n, s, dt=F32: g.sb("rs_" + n, s, dt, inner)
            info = ib("info", [P, KD])
            info2 = ib("info2", [P, KD])
            infob = ib("infob", [P, KD, 16])
            gn = ib("gn", [16, 2])
            mean16 = ib("mean16", [16, 64])
            q = ib("q", [P, KD, GT])
            q2 = ib("q2", [P, KD, GT])
            nr = ib("nr", [16, GT])
            rat = ib("rat", [16, GT])
            sim = ib("sim", [1, B, N])
            lo, hi, span = ib("lo", [1, 1]), ib("hi", [1, 1]), ib("span", [1, 1])
            pos = ib("pos", [1, B, N])
            rows = ib("rows", [1, 2, B, N], BF16)
            krows = ib("krows", [1, 2, B, 2, N], BF16)
            wl, ga, gb, qp, qc, q2s, dt, ns, rs, rt, mn, smp, fin, sent = (g.sem("rs_" + n) for n in (
                "weights", "info_step", "info_product", "q_product", "q_copied", "q_squared", "dots", "norms", "inverse",
                "ratio", "mean_product", "sim_copied", "class_step", "rows_sent"))
            with nc.Block() as block:
                @block.sync
                def _(sp):
                    sp.dma_start(Wqkv[:], feature_rows(A["L0_ffn_W_qkv"])).then_inc(wl, 16)
                    sp.dma_start(info[:], A["L0_info_col"]).then_inc(wl, 16)
                    sp.wait_ge(fin, 15)
                    for r in [32 * quad + c for quad in range(4) for c in range(2)]:
                        sp.dma_start(qm[r:r + 1, :], rows[:, r % 32].rearrange("p b n -> p (b n)")).then_inc(sent, 16)
                        sp.dma_start(km[r:r + 1], krows[:, r % 32]).then_inc(sent, 16)
                    sp.wait_ge(sent, 16 * 16)

                @block.tensor
                def _(pe):
                    pe.wait_ge(ga, 2)
                    for k in range(KD):
                        mm = pe.matmul(g.bank[7][0:16, 0:1], g.c("head16")[:, 16 * k:16 * k + 16], info2[:, k:k + 1],
                                       start=(k == 0), stop=(k == KD - 1))
                    mm.then_inc(gb, 1)
                    pe.wait_ge(ga, 6)
                    with pe.Fori(0, NG) as gi:
                        for m in range(KD):
                            for k in range(KD):
                                mm = pe.matmul(g.bank[m][:], Wqkv[:, k, m * P:(m + 1) * P],
                                               g.XN[:, k, ds(gi * GT, GT)], start=(k == 0), stop=(k == KD - 1))
                        mm.then_inc(qp, 1)
                        pe.wait_ge(qc, gi + 1)
                        for k in range(KD):
                            mm = pe.matmul(g.bank[2][0:16, :], infob[:, k], q[:, k], start=(k == 0), stop=(k == KD - 1))
                        mm.then_inc(dt, 1)
                        pe.wait_ge(q2s, gi + 1)
                        for k in range(KD):
                            mm = pe.matmul(g.bank[3][0:16, :], g.c("head16")[:, 16 * k:16 * k + 16], q2[:, k],
                                           start=(k == 0), stop=(k == KD - 1))
                        mm.then_inc(dt, 1)
                        pe.wait_ge(rt, 2 * gi + 2)
                        pe.matmul(g.bank[4][0:64, :], mean16[:], rat[:], start=True, stop=True).then_inc(mn, 1)

                @block.scalar
                def _(act):
                    act.wait_ge(gb, 1)
                    act.activation(gn[:, 0:1], g.bank[7][0:16, 0:1], ACT.Sqrt).then_inc(ga, 1)
                    with act.Fori(0, NG) as gi:
                        act.wait_ge(qc, gi + 1)
                        for m in range(KD):
                            a = act.activation(q2[:, m], q[:, m], ACT.Square)
                        a.then_inc(q2s, 1)
                        act.wait_ge(dt, 2 * gi + 2)
                        act.activation(nr[:], g.bank[3][0:16, :], ACT.Sqrt).then_inc(ns, 1)
                        act.wait_ge(smp, gi + 1)

                @block.vector
                def _(v):
                    v.wait_ge(wl, 32)
                    v.memset(mean16[:], 1.0 / 16).then_inc(ga, 1)
                    v.tensor_tensor(info2[:], info[:], info[:], ALU.mult).then_inc(ga, 1)
                    for k in range(KD):
                        v.tensor_scalar(infob[:, k], g.c("head16")[:, 16 * k:16 * k + 16], info[:, k:k + 1], None,
                                        ALU.mult).then_inc(ga, 1)
                    v.wait_ge(ga, 5)
                    v.reciprocal(gn[:, 1:2], gn[:, 0:1]).then_inc(ga, 1)
                    v.wait_ge(ga, 6)
                    with v.Fori(0, NG) as gi:
                        v.wait_ge(qp, gi + 1)
                        for m in range(KD):
                            c = v.tensor_copy(q[:, m], g.bank[m][:])
                        c.then_inc(qc, 1)
                        v.wait_ge(ns, gi + 1)
                        v.reciprocal(nr[:], nr[:]).then_inc(rs, 1)
                        v.wait_ge(rs, gi + 1)
                        v.wait_ge(dt, 2 * gi + 2)
                        v.tensor_tensor(rat[:], g.bank[2][0:16, :], nr[:], ALU.mult).then_inc(rt, 1)
                        v.wait_ge(rt, 2 * gi + 1)
                        v.tensor_scalar(rat[:], rat[:], gn[:, 1:2], None, ALU.mult).then_inc(rt, 1)
                        v.wait_ge(mn, gi + 1)
                        v.tensor_copy(sim[:].rearrange("p b n -> p (b n)")[:, ds(gi * GT, GT)], g.bank[4][0:1, :])\
                         .then_inc(smp, 1)
                        v.wait_ge(smp, gi + 1)
                    tok = sim[:, :, REG:N]
                    v.tensor_reduce(lo[:], tok, AX.XY, ALU.min).then_inc(fin, 1)
                    v.tensor_reduce(hi[:], tok, AX.XY, ALU.max).then_inc(fin, 1)
                    v.wait_ge(fin, 2)
                    v.tensor_tensor(span[:], hi[:], lo[:], ALU.subtract).then_inc(fin, 1)
                    v.wait_ge(fin, 3)
                    v.reciprocal(span[:], span[:]).then_inc(fin, 1)
                    v.wait_ge(fin, 4)
                    v.tensor_scalar(pos[:], sim[:], lo[:], span[:], ALU.subtract, ALU.mult).then_inc(fin, 1)
                    v.wait_ge(fin, 5)
                    v.tensor_scalar(pos[:], pos[:], 0.9, None, ALU.is_gt).then_inc(fin, 1)
                    v.wait_ge(fin, 6)
                    v.memset(pos[:, :, 0:REG], 1.0).then_inc(fin, 1)
                    v.wait_ge(fin, 7)
                    v.tensor_copy(rows[:, 0], pos[:]).then_inc(fin, 1)
                    v.tensor_scalar(rows[:, 1], pos[:], -1.0, 1.0, ALU.mult, ALU.add).then_inc(fin, 1)
                    v.wait_ge(fin, 9)
                    for r in range(2):
                        v.tensor_scalar(krows[:, 0, :, r], rows[:, 1], -BIG, None, ALU.mult).then_inc(fin, 1)
                        v.tensor_scalar(krows[:, 1, :, r], rows[:, 0], -BIG, None, ALU.mult).then_inc(fin, 1)
                    v.wait_ge(fin, 13)
                    v.memset(krows[:, 0, :, :, 0:REG], 0.0).then_inc(fin, 1)
                    v.memset(krows[:, 1, :, :, 0:REG], 0.0).then_inc(fin, 1)
        Wp = sb("Wp", [P, KD, D])
        bias = sb("bias", [P, KD])
        qz = sb("qz", [P, 2, KD, N])
        kk = sb("k", [P, KD, N])
        vv = sb("v", [P, 2, D])
        rmask = sb("rmask", [2, 16 * REG], BF16)
        qmb = sb("qmb", [P, N], BF16)
        kmb = sb("kmb", [P, 2, N], BF16)
        made = g.sem("ra_made")
        with nc.Block() as block:
            @block.vector
            def _(v):
                v.memset(rmask[:], 1.0).then_inc(made, 1)
                v.wait_ge(made, 1)
                v.memset(rmask[0:1], 0.0).then_inc(made, 1)

        def weights(sp):
            yield sp.dma_start(Wp[:], feature_rows(A["L0_ffn_W_proj"]))
            yield sp.dma_start(bias[:], A["L0_ffn_b_proj_col"])

        front = qkv_front(Wqkv, kk, vv, own_keys=lambda j: kk[:], own_values=lambda j: vv[:], odd_even=(qz, g.c("even16")))

        def q_of(h, i, j):
            r, s = h // 8, 32 * ((h % 8) // 2)
            return qz[s:s + 32, h % 2, r, i * P:(i + 1) * P]

        def k_of(h, i, j):
            s = 32 * ((h % 8) // 2)
            return kk[s:s + 32, h // 8, :]

        def mask(i, b, hs):
            r = 32 * ((hs[0] % 8) // 2)
            return qmb[r:r + 2, i * P:(i + 1) * P], kmb[r:r + 2].rearrange("c r n -> c (r n)")

        def gather(po, b, xb):
            yield po.tensor_copy(xb[:], g.XN[:, :, ds(b * N, N)])
            for r in range(0, P, 32):
                yield po.tensor_copy(qmb[r:r + 2], qm[r:r + 2, ds(b * N, N)])
                yield po.tensor_copy(kmb[r:r + 2], km[r:r + 2, ds(b, 1)].rearrange("c o r n -> c (o r) n"))

        reg = {"q_mask": rmask[:], "k_mask": lambda b: kmb[0:2, 0],
               "k": lambda k: kk[:, k], "v": lambda c: vv[:, c], "q": lambda s: qz[:, s, :, 0:REG]}
        attention_block(g, ctx, "ra", 16, 16, 2, N, None, front, q_of, k_of,
                        lambda h, c, i, j: vv[:, c, h * 16:(h + 1) * 16],
                        project(Wp, KD), add_to_stream(g, bias), mask=mask, reg=reg, weights=weights, n_weights=2,
                        gather=gather, n_gather=9)


def project(W, chunks):
    def wout(pe, M, outT, xb):
        for m in range(KD):
            for k in range(chunks):
                mm = pe.matmul(M[:, m * N:(m + 1) * N], W[:, k, m * P:(m + 1) * P], outT[:, k],
                               start=(k == 0), stop=(k == chunks - 1))
        return mm
    return wout


def add_to_stream(g, bias):
    def finish(v, M, xb, b):
        for m in range(KD):
            x = g.X[:, m, ds(b * N, N)]
            f = v.scalar_tensor_tensor(x, M[:, m * N:(m + 1) * N], bias[:, m:m + 1], x, ALU.add, ALU.add)
        return f
    return finish


def qkv_front(Wqkv, kk, vv, own_keys, own_values, odd_even):
    qz, even = odd_even
    front = []
    for m in range(2 * KD):
        def product(pe, bank, j, b, xb, m=m):
            for k in range(KD):
                mm = pe.matmul(bank[:, 0:N], Wqkv[:, k, m * P:(m + 1) * P], xb[:, k], start=(k == 0), stop=(k == KD - 1))
            return mm

        def take(eng, bank, j, b, m=m):
            if m < KD:
                for s in range(2):
                    o = eng.tensor_scalar(qz[:, s, m], bank[:, 0:N], even[:, s:s + 1], None, ALU.mult)
                return o
            return eng.activation(own_keys(j)[:, m - KD], bank[:, 0:N], ACT.Copy)
        front.append(("v" if m < KD else "a", product, take))
    for t in range(2):
        def product(pe, bank, j, b, xb, t=t):
            for k in range(KD):
                mm = pe.matmul(bank[:, 0:D], xb[:, k, t * P:(t + 1) * P], Wqkv[:, k, 2 * D:3 * D],
                               start=(k == 0), stop=(k == KD - 1))
            return mm

        def take(eng, bank, j, b, t=t):
            return eng.tensor_copy(own_values(j)[:, t], bank[:, 0:D])
        front.append(("v", product, take))
    return front



def context_attention_layer(g):
    nc, A = g.nc, g.A
    with ExitStack() as ctx:
        sb = lambda n, s, dt=F32: g.sb("ca_" + n, s, dt, ctx)
        Wqkv = sb("Wqkv", [P, KD, 3 * D])
        Wp = sb("Wp", [P, KD, D])
        bias = sb("bias", [P, KD])
        qz = sb("qz", [P, 2, KD, N])
        kk = sb("k", [P, 2, KD, 2 * N])
        vv = sb("v", [P, 2, 4, D])

        def weights(sp):
            yield sp.dma_start(Wqkv[:], feature_rows(A["L1_xattn_w_qkv"]))
            yield sp.dma_start(Wp[:], feature_rows(A["L1_xattn_w_proj"]))
            yield sp.dma_start(bias[:], A["L1_xattn_b_proj_col"])

        def load(sp, b, j):
            yield sp.dma_start(kk[:, j, :, 0:N], feature_rows(A["ctx"][0:D, ds(b * N, N)]))
            yield sp.dma_start(vv[:, j, 0:2], A["ctx_tok"][ds(b * N, N), D:2 * D].rearrange("(t p) d -> p t d", p=P))

        front = qkv_front(Wqkv, kk, vv, own_keys=lambda j: kk[:, j, :, N:2 * N], own_values=lambda j: vv[:, j, 2:4],
                          odd_even=(qz, g.c("even16")))

        def q_of(h, i, j):
            s = 32 * ((h % 8) // 2)
            return qz[s:s + 32, h % 2, h // 8, i * P:(i + 1) * P]

        def k_of(h, i, j):
            s = 32 * ((h % 8) // 2)
            return kk[s:s + 32, j, h // 8, :]

        attention_block(g, ctx, "ca", 16, 16, 1, 2 * N, load, front, q_of, k_of,
                        lambda h, c, i, j: vv[:, j, c, h * 16:(h + 1) * 16],
                        project(Wp, KD), add_to_stream(g, bias), weights=weights, n_weights=3, n_loads=2)



def routed_ffn_layer(g):
    nc, A = g.nc, g.A
    E, WIDTHS = 8, [256] * 4 + [512] * 4
    TW = sum(WIDTHS)
    CH = TW // P
    RS = 28
    expert = [e for e, w in enumerate(WIDTHS) for _ in range(w // P)]
    ident = g.c("ident")
    with ExitStack() as ctx:
        sb = lambda n, s, dt=F32: g.sb("rf_" + n, s, dt, ctx)
        W1 = sb("W1", [P, KD, TW])
        W2 = sb("W2", [P, CH, D])
        Wr = sb("Wr", [P, KD, E])
        xg = sb("xg", [P, KD, GT])
        ex = sb("ex", [P, 4, E])
        pr = sb("pr", [P, 4, E])
        top = sb("top", [P, 4, 8])
        idx = sb("idx", [P, 4, 8], U32)
        idf = sb("idf", [P, 4, 8])
        den = sb("den", [P, 4])
        comb = sb("comb", [P, 4, E])
        comb2 = sb("comb2", [P, 4, E])
        cw = sb("cw", [P, E, GT])
        r = sb("r", [P, 3, GT])
        rc = sb("rc", [P, 3, GT])
        hh = sb("hh", [P, 3, GT])
        wl, xc, rp, ee, rv, cp, cc, hp, ra, rcd, hd, y, done = (g.sem("rf_" + n) for n in (
            "weights", "group_copied", "logits", "exp", "route_step", "spread", "spread_copied", "hidden", "relu",
            "weighted", "squared", "output", "group_done"))
        with nc.Block() as block:
            @block.sync
            def _(sp):
                sp.dma_start(Wr[:], feature_rows(A["L1_ffn_router_w"])).then_inc(wl, 16)
                sp.dma_start(W1[:], feature_rows(A["L1_ffn_w1"])).then_inc(wl, 16)
                sp.dma_start(W2[:], feature_rows(A["L1_ffn_w2"])).then_inc(wl, 16)
                sp.wait_ge(wl, 48)

            @block.gpsimd
            def _(po):
                with po.Fori(0, NG) as gi:
                    po.tensor_copy(xg[:], g.XN[:, :, ds(gi * GT, GT)]).then_inc(xc, 1)
                    for c in range(CH):
                        po.wait_ge(ra, CH * gi + c + 1)
                        if c == 0:
                            po.wait_ge(cc, E * gi + E)
                        if c >= 3:
                            po.wait_ge(hd, CH * gi + c - 2)
                        po.tensor_tensor(rc[:, c % 3], r[:, c % 3], cw[:, expert[c]], ALU.mult).then_inc(rcd, 1)
                        po.wait_ge(rcd, CH * gi + c + 1)
                    po.wait_ge(done, gi + 1)

            @block.tensor
            def _(pe):
                pe.wait_ge(wl, 48)
                with pe.Fori(0, NG) as gi:
                    pe.wait_ge(xc, gi + 1)
                    for t in range(4):
                        for k in range(KD):
                            mm = pe.matmul(g.bank[0][:, t * E:(t + 1) * E], xg[:, k, t * P:(t + 1) * P], Wr[:, k],
                                           start=(k == 0), stop=(k == KD - 1))
                    mm.then_inc(rp, 1)
                    pe.wait_ge(rv, RS * gi + RS)
                    for e in range(E):
                        if e >= 2:
                            pe.wait_ge(cc, E * gi + e - 1)
                        for t in range(4):
                            mm = pe.matmul(g.bank[e % 2][:, t * P:(t + 1) * P],
                                           comb[:, t, e:e + 1].to_broadcast([P, P]), ident, start=True, stop=True)
                        mm.then_inc(cp, 1)

                    def out(c):
                        pe.wait_ge(hd, CH * gi + c + 1)
                        for m in range(KD):
                            mm = pe.matmul(g.bank[6 + m][:], W2[:, c, m * P:(m + 1) * P], hh[:, c % 3],
                                           start=(c == 0), stop=(c == CH - 1), skip_group_check=True)
                        mm.then_inc(y, 1)
                    for c in range(CH):
                        if c >= 3:
                            pe.wait_ge(ra, CH * gi + c - 2)
                        for k in range(KD):
                            mm = pe.matmul(g.bank[2 + c % 3][:], W1[:, k, c * P:(c + 1) * P], xg[:, k],
                                           start=(k == 0), stop=(k == KD - 1))
                        mm.then_inc(hp, 1)
                        if c >= 2:
                            out(c - 2)
                    out(CH - 2)
                    out(CH - 1)
                    pe.wait_ge(done, gi + 1)

            @block.scalar
            def _(act):
                with act.Fori(0, NG) as gi:
                    act.wait_ge(rp, gi + 1)
                    act.activation(ex[:].rearrange("p t e -> p (t e)"), g.bank[0][:, 0:4 * E], ACT.Exp, scale=-1.0)\
                       .then_inc(ee, 1)
                    for e in range(E):
                        act.wait_ge(cp, E * gi + e + 1)
                        act.activation(cw[:, e], g.bank[e % 2][:], ACT.Copy).then_inc(cc, 1)
                    for c in range(CH):
                        act.wait_ge(hp, CH * gi + c + 1)
                        if c >= 3:
                            act.wait_ge(hd, CH * gi + c - 2)
                        act.activation(r[:, c % 3], g.bank[2 + c % 3][:], ACT.Relu).then_inc(ra, 1)
                    act.wait_ge(done, gi + 1)

            @block.vector
            def _(v):
                with v.Fori(0, NG) as gi:
                    v.wait_ge(ee, gi + 1)
                    v.tensor_scalar(ex[:], ex[:], 1.0, None, ALU.add).then_inc(rv, 1)
                    v.wait_ge(rv, RS * gi + 1)
                    v.reciprocal(pr[:], ex[:]).then_inc(rv, 1)
                    v.wait_ge(rv, RS * gi + 2)
                    for t in range(4):
                        v.memset(g.hold[:], 0.0)
                        v.max(top[:, t], pr[:, t]).then_inc(rv, 1)
                        v.wait_ge(rv, RS * gi + 2 + 2 * t + 1)
                        v.memset(g.hold[:], 0.0)
                        v.max_index(idx[:, t], top[:, t], pr[:, t]).then_inc(rv, 1)
                        v.wait_ge(rv, RS * gi + 2 + 2 * t + 2)
                    v.tensor_copy(idf[:], idx[:]).then_inc(rv, 1)
                    v.tensor_tensor(den[:], top[:, :, 0], top[:, :, 1], ALU.add).then_inc(rv, 1)
                    v.wait_ge(rv, RS * gi + 12)
                    v.tensor_scalar(den[:], den[:], 1e-20, None, ALU.add).then_inc(rv, 1)
                    v.wait_ge(rv, RS * gi + 13)
                    v.reciprocal(den[:], den[:]).then_inc(rv, 1)
                    v.wait_ge(rv, RS * gi + 14)
                    for n in range(2):
                        v.tensor_tensor(top[:, :, n], top[:, :, n], den[:], ALU.mult).then_inc(rv, 1)
                    v.wait_ge(rv, RS * gi + 16)
                    for t in range(4):
                        v.tensor_scalar(comb[:, t], g.c("iota8"), idf[:, t, 0:1], top[:, t, 0:1],
                                        ALU.is_equal, ALU.mult).then_inc(rv, 1)
                        v.tensor_scalar(comb2[:, t], g.c("iota8"), idf[:, t, 1:2], top[:, t, 1:2],
                                        ALU.is_equal, ALU.mult).then_inc(rv, 1)
                        v.wait_ge(rv, RS * gi + 16 + 3 * t + 2)
                        v.tensor_tensor(comb[:, t], comb[:, t], comb2[:, t], ALU.add).then_inc(rv, 1)
                    for c in range(CH):
                        v.wait_ge(rcd, CH * gi + c + 1)
                        if c >= 3:
                            v.wait_ge(y, CH * gi + c - 2)
                        v.tensor_tensor(hh[:, c % 3], rc[:, c % 3], r[:, c % 3], ALU.mult).then_inc(hd, 1)
                    v.wait_ge(y, CH * gi + CH)
                    for m in range(KD):
                        x = g.X[:, m, ds(gi * GT, GT)]
                        f = v.tensor_tensor(x, g.bank[6 + m][:], x, ALU.add)
                    f.then_inc(done, 1)
                    v.wait_ge(done, gi + 1)



def null_attention_layer(g):
    nc, A = g.nc, g.A
    H, DH = 16, 64
    INNER = H * DH
    IC = INNER // P
    with ExitStack() as outer:
        gain = g.sb("na_gain", [P, KD], F32, outer)
        shift = g.sb("na_shift", [P, KD], F32, outer)
        with ExitStack() as ctx:
            sb = lambda n, s, dt=F32: g.sb("na_" + n, s, dt, ctx)
            Wq = sb("Wq", [P, KD, INNER])
            Wkv = sb("Wkv", [P, KC, 2 * INNER])
            Wo = sb("Wo", [P, IC, D])
            cxT = sb("cxT", [P, 2, KC, N])
            qq = sb("q", [P, IC, N])
            kk = sb("k", [P, IC, N + 1])
            vv = sb("v", [P, 2, INNER])
            nv = sb("nv", [H, INNER])
            nk = sb("nk", [P, IC])
            nkl, zeroed = g.sem("na_null_loaded"), g.sem("na_zeroed")
            with nc.Block() as block:
                @block.sync
                def _(sp):
                    for half in range(2):
                        sp.dma_start(nk[half * DH:(half + 1) * DH, :], A["L2_null_key"]).then_inc(nkl, 16)

                @block.vector
                def _(v):
                    v.memset(nv[:], 0.0).then_inc(zeroed, 1)
                    v.wait_ge(nkl, 32)
                    v.tensor_copy(kk[:, :, N], nk[:]).then_inc(zeroed, 1)

            def weights(sp):
                yield sp.dma_start(Wq[:], feature_rows(A["L2_xattn_Wq"]))
                yield sp.dma_start(Wkv[:], feature_rows(A["L2_xattn_Wkv"]))
                yield sp.dma_start(Wo[:], feature_rows(A["L2_xattn_Wout"]))
                yield sp.dma_start(gain[:], A["L2_xattn_ln_scale_col"])
                yield sp.dma_start(shift[:], A["L2_xattn_ln_bias_col"])
                for h in range(H):
                    yield sp.dma_start(nv[h:h + 1, h * DH:(h + 1) * DH], A["L2_xattn_null_kv"][1:2, :])

            def load(sp, b, j):
                yield sp.dma_start(cxT[:, j], feature_rows(A["ctx"][:, ds(b * N, N)]))

            front = []
            for m in range(IC):
                def q_product(pe, bank, j, b, xb, m=m):
                    for k in range(KD):
                        mm = pe.matmul(bank[:, 0:N], Wq[:, k, m * P:(m + 1) * P], xb[:, k],
                                       start=(k == 0), stop=(k == KD - 1))
                    return mm

                def q_take(eng, bank, j, b, m=m):
                    return eng.tensor_scalar(qq[:, m], bank[:, 0:N], DH ** -0.5, None, ALU.mult)

                def k_product(pe, bank, j, b, xb, m=m):
                    for k in range(KC):
                        mm = pe.matmul(bank[:, 0:N], Wkv[:, k, m * P:(m + 1) * P], cxT[:, j, k],
                                       start=(k == 0), stop=(k == KC - 1))
                    return mm

                def k_take(eng, bank, j, b, m=m):
                    return eng.activation(kk[:, m, 0:N], bank[:, 0:N], ACT.Copy)
                front += [("v", q_product, q_take), ("a", k_product, k_take)]
            for t in range(2):
                for half in range(2):
                    def v_product(pe, bank, j, b, xb, t=t, half=half):
                        for k in range(KC):
                            mm = pe.matmul(bank[:], cxT[:, j, k, t * P:(t + 1) * P],
                                           Wkv[:, k, INNER + half * 512:INNER + (half + 1) * 512],
                                           start=(k == 0), stop=(k == KC - 1))
                        return mm

                    def v_take(eng, bank, j, b, t=t, half=half):
                        return eng.tensor_copy(vv[:, t, half * 512:(half + 1) * 512], bank[:])
                    front.append(("v", v_product, v_take))

            def finish(v, M, xb, b):
                return v.tensor_copy(g.XN[:, :, ds(b * N, N)], M[:].rearrange("p (m n) -> p m n", m=KD))

            attention_block(g, ctx, "na", H, DH, 1, N + 1, load, front,
                            lambda h, i, j: qq[(h % 2) * DH:(h % 2 + 1) * DH, h // 2, i * P:(i + 1) * P],
                            lambda h, i, j: kk[(h % 2) * DH:(h % 2 + 1) * DH, h // 2, :],
                            lambda h, c, i, j: vv[:, c, h * DH:(h + 1) * DH],
                            project(Wo, IC), finish, null=nv, weights=weights, n_weights=5 + H, n_loads=1)
        layer_norm_phase(g, "nax", src=g.XN, dst=g.X, gain=gain, shift=shift, resid=g.X, eps=g.eps6)



def split3(v, x, parts, step, at):
    v.tensor_copy(parts[0], x).then_inc(step, 1)
    v.wait_ge(step, at + 1)
    v.tensor_tensor(x, x, parts[0], ALU.subtract).then_inc(step, 1)
    v.wait_ge(step, at + 2)
    v.tensor_copy(parts[1], x).then_inc(step, 1)
    v.wait_ge(step, at + 3)
    return v.tensor_tensor(parts[2], x, parts[1], ALU.subtract)


def sign_ffn_layer(g):
    nc, A = g.nc, g.A
    F1, F2 = 1024, 1024
    C1, C2 = F1 // P, F2 // P
    with ExitStack() as ctx:
        sb = lambda n, s, dt=F32: g.sb("sf_" + n, s, dt, ctx)
        W0 = sb("W0", [P, KD, F1], BF16)
        W1 = sb("W1", [P, C1, F2], BF16)
        W2 = sb("W2", [P, C2, D], BF16)
        sc = sb("sc", [P, 3])
        with ExitStack() as inner:
            ib = lambda n, s, dt=F32: g.sb("sk_" + n, s, dt, inner)
            k0 = ib("k0", [P, 2 * KD, F1 // 4], I32)
            k1 = ib("k1", [P, C1, F2 // 4], I32)
            k2 = ib("k2", [P, C2, D // 4], I32)
            dif = ib("dif", [P, KD, F1])
            wl, st = g.sem("sk_loaded"), g.sem("sk_step")
            with nc.Block() as block:
                @block.sync
                def _(sp):
                    sp.dma_start(k0[:], feature_rows(A["L2_ffn_k0"])).then_inc(wl, 16)
                    sp.dma_start(k1[:], feature_rows(A["L2_ffn_k1"])).then_inc(wl, 16)
                    sp.dma_start(k2[:], feature_rows(A["L2_ffn_k2"])).then_inc(wl, 16)
                    for n in range(3):
                        sp.dma_start(sc[:, n:n + 1], A[f"L2_ffn_s{n}"].unsqueeze(0).to_broadcast([P, 1])).then_inc(wl, 16)
                    sp.wait_ge(wl, 96)

                @block.vector
                def _(v):
                    v.wait_ge(wl, 96)
                    b0 = k0[:].bitcast(U8)
                    v.tensor_tensor(dif[:], b0[:, 0:KD], b0[:, KD:2 * KD], ALU.subtract).then_inc(st, 1)
                    v.wait_ge(st, 1)
                    v.tensor_scalar(W0[:], dif[:], 2.0, None, ALU.mult).then_inc(st, 1)
                    v.tensor_scalar(W1[:], k1[:].bitcast(U8), 2.0, -1.0, ALU.mult, ALU.add).then_inc(st, 1)
                    v.tensor_scalar(W2[:], k2[:].bitcast(U8), 2.0, -1.0, ALU.mult, ALU.add).then_inc(st, 1)
                    v.tensor_scalar(sc[:, 0:2], sc[:, 0:2], 2.0, None, ALU.mult).then_inc(st, 1)
        xf = sb("xf", [P, KD, GT])
        xs = sb("xs", [P, 3, KD, GT], BF16)
        hf = sb("hf", [P, 4, GT])
        h1 = sb("h1", [P, C1, 3, GT], BF16)
        h2 = sb("h2", [P, C2, 3, GT], BF16)
        xc, st, sp0, hp, ha, s1, hs, y, done = (g.sem("sf_" + n) for n in (
            "group_copied", "x_split", "x_parts", "hidden", "relu", "h_split", "h_parts", "output", "group_done"))
        CT = C1 + C2
        with nc.Block() as block:
            @block.gpsimd
            def _(po):
                with po.Fori(0, NG) as gi:
                    po.tensor_copy(xf[:], g.XN[:, :, ds(gi * GT, GT)]).then_inc(xc, 1)
                    po.wait_ge(done, gi + 1)

            @block.tensor
            def _(pe):
                with pe.Fori(0, NG) as gi:
                    pe.wait_ge(sp0, gi + 1)
                    for c in range(CT):
                        if c >= 4:
                            pe.wait_ge(ha, CT * gi + c - 3)
                        if c < C1:
                            for k in range(KD):
                                for s in range(3):
                                    mm = pe.matmul(g.bank[c % 4][:], W0[:, k, c * P:(c + 1) * P], xs[:, s, k],
                                                   start=(k == 0 and s == 0), stop=(k == KD - 1 and s == 2))
                        else:
                            m = c - C1
                            for k in range(C1):
                                if m == 0:
                                    pe.wait_ge(hs, CT * gi + k + 1)
                                for s in range(3):
                                    mm = pe.matmul(g.bank[c % 4][:], W1[:, k, m * P:(m + 1) * P], h1[:, k, s],
                                                   start=(k == 0 and s == 0), stop=(k == C1 - 1 and s == 2))
                        mm.then_inc(hp, 1)
                    for k in range(C2):
                        pe.wait_ge(hs, CT * gi + C1 + k + 1)
                        for m in range(KD):
                            for s in range(3):
                                mm = pe.matmul(g.bank[6 + m][:], W2[:, k, m * P:(m + 1) * P], h2[:, k, s],
                                               start=(k == 0 and s == 0), stop=(k == C2 - 1 and s == 2))
                    mm.then_inc(y, 1)
                    pe.wait_ge(done, gi + 1)

            @block.scalar
            def _(act):
                with act.Fori(0, NG) as gi:
                    for c in range(CT):
                        act.wait_ge(hp, CT * gi + c + 1)
                        if c >= 4:
                            act.wait_ge(hs, CT * gi + c - 3)
                        n = 0 if c < C1 else 1
                        act.activation(hf[:, c % 4], g.bank[c % 4][:], ACT.Relu, scale=sc[:, n:n + 1]).then_inc(ha, 1)
                    act.wait_ge(done, gi + 1)

            @block.vector
            def _(v):
                with v.Fori(0, NG) as gi:
                    v.wait_ge(xc, gi + 1)
                    split3(v, xf[:], [xs[:, s] for s in range(3)], st, 3 * gi).then_inc(sp0, 1)
                    for c in range(CT):
                        v.wait_ge(ha, CT * gi + c + 1)
                        dst = h1[:, c] if c < C1 else h2[:, c - C1]
                        split3(v, hf[:, c % 4], [dst[:, s] for s in range(3)], s1, 3 * (CT * gi + c)).then_inc(hs, 1)
                    v.wait_ge(y, gi + 1)
                    for m in range(KD):
                        x = g.X[:, m, ds(gi * GT, GT)]
                        f = v.scalar_tensor_tensor(x, g.bank[6 + m][:], sc[:, 2:3], x, ALU.mult, ALU.add)
                    f.then_inc(done, 1)
                    v.wait_ge(done, gi + 1)



def masked_attention_layer(g):
    nc, A = g.nc, g.A
    H, DH = 8, 32
    with ExitStack() as ctx:
        sb = lambda n, s, dt=F32: g.sb("ma_" + n, s, dt, ctx)
        Ws = sb("Ws", [P, KC, 2 * D])
        Wt = sb("Wt", [P, KD, D])
        Wo = sb("Wo", [P, 2 * KD, D])
        bs = sb("bs", [P, 4])
        bt = sb("bt", [P, KD])
        bo = sb("bo", [P, KD])
        bv = sb("bv", [1, D])
        mrow = sb("mrow", [P, T])
        mrows = sb("mrows", [P, T])
        mcol = sb("mcol", [P, T // P])
        drop = sb("drop", [P, T], BF16)
        mb = sb("mb", [P, N])
        mbs = sb("mbs", [P, N])
        mbc = sb("mbc", [P, 2])
        dropb = sb("dropb", [P, 2, N], BF16)
        cxT = sb("cxT", [P, 2, KC, N])
        qq = sb("q", [P, KD, N])
        kk = sb("k", [P, KD, N])
        vv = sb("v", [P, 2, D])
        wl, st = g.sem("mk_loaded"), g.sem("mk_step")
        with nc.Block() as block:
            @block.sync
            def _(sp):
                m1 = A["mask_BxS2_fk1"].rearrange("b n -> (b n)")
                sp.dma_start(mrow[:], m1.unsqueeze(0).to_broadcast([P, T])).then_inc(wl, 16)
                sp.dma_start(mcol[:], A["mask_col"]).then_inc(wl, 16)
                sp.wait_ge(wl, 32)

            @block.vector
            def _(v):
                v.wait_ge(wl, 32)
                v.tensor_scalar(drop[:], mrow[:], 0.0, -BIG, ALU.is_equal, ALU.mult).then_inc(st, 1)
                v.tensor_scalar(mrows[:], mrow[:], DH ** -0.5, None, ALU.mult).then_inc(st, 1)

        def weights(sp):
            for t, name in ((Ws, "L3_xattn_W_src"), (Wt, "L3_xattn_W_tgt"), (Wo, "L3_xattn_W_out")):
                yield sp.dma_start(t[:], feature_rows(A[name]))
            yield sp.dma_start(bs[:], A["L3_xattn_b_src_col"])
            yield sp.dma_start(bt[:], A["L3_xattn_b_tgt_col"])
            yield sp.dma_start(bo[:], A["L3_xattn_b_out_col"])
            yield sp.dma_start(bv[:], A["L3_xattn_b_src"][D:2 * D].unsqueeze(0))

        def load(sp, b, j):
            yield sp.dma_start(cxT[:, j], feature_rows(A["ctx"][:, ds(b * N, N)]))

        def gather(po, b, xb):
            yield po.tensor_copy(xb[:], g.XN[:, :, ds(b * N, N)])
            yield po.tensor_copy(mb[:], mrow[:, ds(b * N, N)])
            yield po.tensor_copy(mbs[:], mrows[:, ds(b * N, N)])
            yield po.tensor_copy(mbc[:], mcol[:, ds(b * 2, 2)])
            for r in range(2):
                yield po.tensor_copy(dropb[:, r], drop[:, ds(b * N, N)])

        front = []
        for m in range(KD):
            def q_product(pe, bank, j, b, xb, m=m):
                for k in range(KD):
                    mm = pe.matmul(bank[:, 0:N], Wt[:, k, m * P:(m + 1) * P], xb[:, k], start=(k == 0), stop=(k == KD - 1))
                return mm

            def q_take(eng, bank, j, b, m=m):
                return eng.scalar_tensor_tensor(qq[:, m], bank[:, 0:N], bt[:, m:m + 1], mbs[:], ALU.add, ALU.mult)

            def k_product(pe, bank, j, b, xb, m=m):
                for k in range(KC):
                    mm = pe.matmul(bank[:, 0:N], Ws[:, k, m * P:(m + 1) * P], cxT[:, j, k],
                                   start=(k == 0), stop=(k == KC - 1))
                return mm

            def k_take(eng, bank, j, b, m=m):
                return eng.scalar_tensor_tensor(kk[:, m], bank[:, 0:N], bs[:, m:m + 1], mb[:], ALU.add, ALU.mult)
            front += [("v", q_product, q_take), ("v", k_product, k_take)]
        for t in range(2):
            def v_product(pe, bank, j, b, xb, t=t):
                pe.matmul(bank[:, 0:D], g.c("ones")[0:1, :], bv[:], start=True, stop=False)
                for k in range(KC):
                    mm = pe.matmul(bank[:, 0:D], cxT[:, j, k, t * P:(t + 1) * P], Ws[:, k, D:2 * D],
                                   start=False, stop=(k == KC - 1))
                return mm

            def v_take(eng, bank, j, b, t=t):
                return eng.activation(vv[:, t], bank[:, 0:D], ACT.Copy, scale=mbc[:, t:t + 1])
            front.append(("a", v_product, v_take))

        def mask(i, b, hs):
            r = 32 * (hs[0] % 4)
            return g.onesb[r:r + 1, :], dropb[r:r + 1].rearrange("c r n -> c (r n)")

        def wout(pe, M, outT, xb):
            for m in range(KD):
                for k in range(2 * KD):
                    mm = pe.matmul(M[:, m * N:(m + 1) * N], Wo[:, k, m * P:(m + 1) * P],
                                   xb[:, k] if k < KD else outT[:, k - KD], start=(k == 0), stop=(k == 2 * KD - 1))
            return mm

        attention_block(g, ctx, "ma", H, DH, 2, N, load, front,
                        lambda h, i, j: qq[(h % 4) * DH:(h % 4 + 1) * DH, h // 4, i * P:(i + 1) * P],
                        lambda h, i, j: kk[(h % 4) * DH:(h % 4 + 1) * DH, h // 4, :],
                        lambda h, c, i, j: vv[:, c, h * DH:(h + 1) * DH],
                        wout, add_to_stream(g, bo), mask=mask, weights=weights, n_weights=7, n_loads=1,
                        gather=gather, n_gather=6, wide_gather=True, units=[[h, h + 4] for h in range(4)])



def position_attention_layer(g):
    nc, A = g.nc, g.A
    H, DH, NP = 4, 64, 16
    with ExitStack() as outer:
        gain = g.sb("pa_gain", [P, KD], F32, outer)
        shift = g.sb("pa_shift", [P, KD], F32, outer)
        with ExitStack() as ctx:
            sb = lambda n, s, dt=F32: g.sb("pa_" + n, s, dt, ctx)
            W = sb("W", [P, KD, 3 * D])
            Wo = sb("Wo", [P, KD, D])
            bi = sb("bi", [P, 6])
            bo = sb("bo", [P, KD])
            bv = sb("bv", [1, D])
            qq = sb("q", [P, KD, N])
            kk = sb("k", [P, KD, N])
            vv = sb("v", [P, 2, D])
            pq = sb("pq", [P, P], BF16)
            pk = sb("pk", [P, 2, P], BF16)
            made = g.sem("pa_made")
            with nc.Block() as block:
                @block.vector
                def _(v):
                    for half in range(2):
                        r = 64 * half
                        v.tensor_copy(pq[r:r + NP], g.c("posq")[0:NP, :]).then_inc(made, 1)
                        for c in range(2):
                            v.tensor_copy(pk[r:r + NP, c], g.c("posk")[0:NP, :]).then_inc(made, 1)

            def weights(sp):
                yield sp.dma_start(W[:], feature_rows(A["L3_ffn_in_proj_w"]))
                yield sp.dma_start(Wo[:], feature_rows(A["L3_ffn_out_proj_w"]))
                yield sp.dma_start(bi[:], A["L3_ffn_in_proj_b_col"])
                yield sp.dma_start(bo[:], A["L3_ffn_out_proj_b_col"])
                yield sp.dma_start(bv[:], A["L3_ffn_in_proj_b"][2 * D:3 * D].unsqueeze(0))
                yield sp.dma_start(gain[:], A["L3_ffn_ln1_g_col"])
                yield sp.dma_start(shift[:], A["L3_ffn_ln1_b_col"])

            def tokens(m, i, b):
                return g.XN[:, m].rearrange("p (l n) -> p l n", l=B)[:, :, ds(b * 2 * NP + i * NP, NP)]

            def gather(po, b, xb):
                for m in range(KD):
                    for i in range(2):
                        yield po.tensor_copy(xb[:, m, i * P:(i + 1) * P].rearrange("p (l n) -> p l n", l=B),
                                             tokens(m, i, b))

            front = []
            for m in range(2 * KD):
                def product(pe, bank, j, b, xb, m=m):
                    for k in range(KD):
                        mm = pe.matmul(bank[:, 0:N], W[:, k, m * P:(m + 1) * P], xb[:, k],
                                       start=(k == 0), stop=(k == KD - 1))
                    return mm

                def take(eng, bank, j, b, m=m):
                    if m < KD:
                        return eng.tensor_scalar(qq[:, m], bank[:, 0:N], bi[:, m:m + 1], DH ** -0.5, ALU.add, ALU.mult)
                    return eng.activation(kk[:, m - KD], bank[:, 0:N], ACT.Identity, bias=bi[:, m:m + 1])
                front.append(("v" if m < KD else "a", product, take))
            for t in range(2):
                def v_product(pe, bank, j, b, xb, t=t):
                    pe.matmul(bank[:, 0:D], g.c("ones")[0:1, :], bv[:], start=True, stop=False)
                    for k in range(KD):
                        mm = pe.matmul(bank[:, 0:D], xb[:, k, t * P:(t + 1) * P], W[:, k, 2 * D:3 * D],
                                       start=False, stop=(k == KD - 1))
                    return mm

                def v_take(eng, bank, j, b, t=t):
                    return eng.tensor_copy(vv[:, t], bank[:, 0:D])
                front.append(("v", v_product, v_take))

            def mask(i, b, hs):
                r = 64 * (hs[0] % 2)
                return pq[r:r + NP, :], pk[r:r + NP].rearrange("c r n -> c (r n)")

            def finish(v, M, xb, b):
                for m in range(KD):
                    for i in range(2):
                        c0 = m * N + i * P
                        x = tokens(m, i, b)
                        f = v.scalar_tensor_tensor(x, M[:, c0:c0 + P].rearrange("p (l n) -> p l n", l=B),
                                                   bo[:, m:m + 1], x, ALU.add, ALU.add)
                return f

            def rows(h):
                return slice((h % 2) * DH, (h % 2 + 1) * DH)

            attention_block(g, ctx, "pa", H, DH, 2, P, None, front,
                            lambda h, i, j: qq[rows(h), h // 2, i * P:(i + 1) * P],
                            lambda h, i, j: kk[rows(h), h // 2, i * P:(i + 1) * P],
                            lambda h, c, i, j: vv[:, i, h * DH:(h + 1) * DH],
                            project(Wo, KD), finish, mask=mask, weights=weights, n_weights=7,
                            gather=gather, n_gather=2 * KD, wide_gather=True, units=[[0, 2], [1, 3]])
        layer_norm_phase(g, "npa", src=g.XN, dst=g.XN, gain=gain, shift=shift)



def expert_layer(g):
    nc, A = g.nc, g.A
    E, FF = 8, 1024
    CAP = T // E
    FC = FF // P
    TT = T // P
    ident = g.c("ident")
    with ExitStack() as outer:
        gain = g.sb("xl_gain", [P, KD], F32, outer)
        shift = g.sb("xl_shift", [P, KD], F32, outer)
        sent = nc.dram_tensor("xl_sent", (2 * T, D), F32).ap()
        back = nc.dram_tensor("xl_back", (T, D), F32).ap()
        with ExitStack() as ctx:
            sb = lambda n, s, dt=F32: g.sb("xl_" + n, s, dt, ctx)
            Wg = sb("Wg", [P, KD, E])
            tri = sb("tri", [P, P], BF16)
            slot = sb("slot", [P, TT], U32)
            fetch = sb("fetch", [P, TT], U32)
            gate = sb("gate", [P, TT])
            zero = sb("zero", [P, 4, D])
            xt = sb("xt", [P, KD, P])
            row = sb("row", [P, 2, D])
            carry = sb("carry", [P, E])
            lg = sb("lg", [P, E])
            mx = sb("mx", [P, 8])
            ix = sb("ix", [P, 8], U32)
            ixf = sb("ixf", [P, 8])
            s4 = sb("s4", [P, 8])
            pe8 = sb("pe8", [P, E])
            hot = sb("hot", [P, E])
            hotb = sb("hotb", [P, E], BF16)
            loc = sb("loc", [P, E])
            fl = sb("fl", [P, 4])
            slc = sb("slc", [P, 2], U32)
            wl, zs, xc, lp, st, eg, cp, tp, tc, sc2 = (g.sem("xl_" + n) for n in (
                "weights", "zeroed", "tile_copied", "logits", "route_step", "gate_exp", "counted", "turned",
                "turned_copied", "tile_sent"))
            NV = 20
            with nc.Block() as block:
                @block.sync
                def _(sp):
                    sp.dma_start(Wg[:], feature_rows(A["L3_ffn_wg"])).then_inc(wl, 16)
                    sp.dma_start(gain[:], A["L3_ffn_ln2_g_col"]).then_inc(wl, 16)
                    sp.dma_start(shift[:], A["L3_ffn_ln2_b_col"]).then_inc(wl, 16)
                    sp.wait_ge(st, 1)
                    for n in range(T // (4 * P)):
                        sp.dma_start(sent[n * 4 * P:(n + 1) * 4 * P, :].rearrange("(t p) d -> p t d", p=P), zero[:])\
                          .then_inc(zs, 16)
                    sp.wait_ge(zs, 64)
                    sp.wait_ge(wl, 48)

                @block.scalar
                def _(act):
                    with act.Fori(0, TT) as t:
                        act.wait_ge(st, NV * t + 4 + 3)
                        act.activation(pe8[:], lg[:], ACT.Exp, bias=s4[:, 0:1], accum_out=s4[:, 1:2]).then_inc(eg, 1)
                        act.wait_ge(st, NV * t + 4 + NV)

                @block.tensor
                def _(pe):
                    pe.wait_ge(wl, 48)
                    pe.wait_ge(st, 4)
                    with pe.Fori(0, TT) as t:
                        pe.wait_ge(xc, t + 1)
                        for k in range(KD):
                            mm = pe.matmul(g.bank[0][:, 0:E], xt[:, k], Wg[:, k], start=(k == 0), stop=(k == KD - 1))
                        mm.then_inc(lp, 1)
                        for k in range(KD):
                            mm = pe.transpose(g.bank[1][:, k * P:(k + 1) * P], xt[:, k], ident)
                        mm.then_inc(tp, 1)
                        pe.wait_ge(st, NV * t + 4 + 8)
                        pe.matmul(g.bank[2][:, 0:E], tri[:], hotb[:], start=True, stop=True)
                        pe.matmul(g.bank[2][:, 64:64 + E], g.onesb[:], hotb[:], start=True, stop=True).then_inc(cp, 1)
                        pe.wait_ge(st, NV * t + 4 + NV)

                @block.vector
                def _(v):
                    v.memset(zero[:], 0.0).then_inc(st, 1)
                    v.memset(carry[:], 0.0).then_inc(st, 1)
                    v.tensor_copy(tri[:], g.c("tri")).then_inc(st, 1)
                    v.memset(s4[:], 0.0).then_inc(st, 1)
                    v.wait_ge(st, 4)
                    with v.Fori(0, TT) as t:
                        n = 0

                        def step(o):
                            nonlocal n
                            n += 1
                            o.then_inc(st, 1)
                            v.wait_ge(st, NV * t + 4 + n)
                        v.wait_ge(lp, t + 1)
                        step(v.tensor_copy(lg[:], g.bank[0][:, 0:E]))
                        v.memset(g.hold[:], 0.0)
                        step(v.max(mx[:], lg[:]))
                        step(v.tensor_scalar(s4[:, 0:1], mx[:, 0:1], -1.0, None, ALU.mult))
                        v.memset(g.hold[:], 0.0)
                        step(v.max_index(ix[:], mx[:], lg[:]))
                        step(v.tensor_copy(ixf[:], ix[:]))
                        step(v.tensor_scalar(hot[:], g.c("iota8"), ixf[:, 0:1], None, ALU.is_equal))
                        v.wait_ge(tp, t + 1)
                        step(v.tensor_copy(row[:, 0], g.bank[1][:, 0:D]))
                        step(v.tensor_copy(hotb[:], hot[:]))
                        v.wait_ge(cp, t + 1)
                        step(v.tensor_tensor(loc[:], g.bank[2][:, 0:E], carry[:], ALU.add))
                        step(v.tensor_tensor(carry[:], g.bank[2][:, 64:64 + E], carry[:], ALU.add))
                        step(v.tensor_tensor(loc[:], loc[:], hot[:], ALU.mult))
                        step(v.tensor_reduce(fl[:, 0:1], loc[:], AX.X, ALU.add))
                        step(v.tensor_scalar(fl[:, 1:2], fl[:, 0:1], float(CAP), None, ALU.is_lt))
                        step(v.scalar_tensor_tensor(fl[:, 2:3], ixf[:, 0:1], float(CAP), fl[:, 0:1], ALU.mult, ALU.add))
                        step(v.tensor_tensor(fl[:, 2:3], fl[:, 2:3], fl[:, 1:2], ALU.mult))
                        step(v.tensor_scalar(fl[:, 0:1], fl[:, 1:2], -1.0, 1.0, ALU.mult, ALU.add))
                        step(v.scalar_tensor_tensor(fl[:, 3:4], fl[:, 0:1], g.c("token")[:, ds(t, 1)], fl[:, 2:3],
                                                    ALU.mult, ALU.add))
                        step(v.tensor_copy(slc[:, 0:1], fl[:, 3:4]))
                        v.tensor_copy(fetch[:, ds(t, 1)], fl[:, 2:3])
                        v.wait_ge(eg, t + 1)
                        step(v.reciprocal(s4[:, 2:3], s4[:, 1:2]))
                        step(v.tensor_tensor(gate[:, ds(t, 1)], s4[:, 2:3], fl[:, 1:2], ALU.mult))
                        assert n == NV
                        v.wait_ge(sc2, 16 * t + 16)

                @block.gpsimd
                def _(po):
                    po.wait_ge(zs, 64)
                    with po.Fori(0, TT) as t:
                        po.tensor_copy(xt[:], g.XN[:, :, ds(t * P, P)]).then_inc(xc, 1)
                        po.wait_ge(st, NV * t + 4 + 18)
                        hold_pool(g, po)
                        po.indirect_dma_start(sent, bass.IndirectOffsetOnAxis(ap=slc[:, 0:1], axis=0), row[:, 0], None)\
                          .then_inc(sc2, 16)
                        po.wait_ge(sc2, 16 * t + 16)
                        po.wait_ge(st, NV * t + 4 + NV)

            w1 = sb("w1", [P, 2, KD, FF])
            w2 = sb("w2", [P, 2, FC, D])
            b1 = sb("b1", [P, 2, FC])
            b2 = sb("b2", [1, 2, D])
            xin = sb("xin", [P, 2, 2, D])
            xT = sb("xT", [P, KD, CAP])
            hT = sb("hT", [P, FC, CAP])
            yt = sb("yt", [P, 2, 2, D])
            ld = [g.sem(f"xe_loaded{j}") for j in range(2)]
            so = [g.sem(f"xe_stored{j}") for j in range(2)]
            NL = 5
            tn, tc2, hp, hv, yp, done = (g.sem("xe_" + n) for n in (
                "turned", "turned_copied", "hidden", "hidden_copied", "output", "expert_done"))
            with nc.Block() as block:
                @block.sync
                def _(sp):
                    def load(e, j):
                        for dst, src in (
                                (w1[:, j], A["L3_ffn_w1"][ds(e * D, D), :].rearrange("(k p) f -> p k f", p=P)),
                                (w2[:, j], A["L3_ffn_w2"][ds(e * FF, FF), :].rearrange("(k p) f -> p k f", p=P)),
                                (b1[:, j], A["L3_b1_col"][ds(e * P, P), :]),
                                (b2[:, j], A["L3_ffn_b2"][ds(e, 1), :]),
                                (xin[:, j], sent[ds(e * CAP, CAP), :].rearrange("(t p) d -> p t d", p=P))):
                            sp.dma_start(dst, src).then_inc(ld[j], 16)
                    load(0, 0)
                    load(1, 1)
                    with sp.Fori(0, E // 2 - 1) as pair:
                        for j in range(2):
                            sp.wait_ge(done, 2 * pair + j + 1)
                            load(2 * pair + j + 2, j)

                @block.tensor
                def _(pe):
                    with pe.Fori(0, E // 2) as pair:
                        for j in range(2):
                            e = 2 * pair + j
                            pe.wait_ge(ld[j], 16 * NL * pair + 16 * NL)
                            for k in range(KD):
                                for t in range(2):
                                    mm = pe.transpose(g.bank[0][:, k * CAP + t * P:k * CAP + (t + 1) * P],
                                                      xin[:, j, t, k * P:(k + 1) * P], ident)
                            mm.then_inc(tn, 1)
                            pe.wait_ge(tc2, e + 1)
                            for c in range(FC):
                                if c >= 4:
                                    pe.wait_ge(hv, FC * e + c - 3)
                                for k in range(KD):
                                    mm = pe.matmul(g.bank[1 + c % 4][:, 0:CAP], w1[:, j, k, c * P:(c + 1) * P], xT[:, k],
                                                   start=(k == 0), stop=(k == KD - 1))
                                mm.then_inc(hp, 1)
                            for t in range(2):
                                pe.matmul(g.bank[5 + t][:, 0:D], g.c("ones")[0:1, :], b2[:, j], start=True, stop=False)
                                for c in range(FC):
                                    if t == 0:
                                        pe.wait_ge(hv, FC * e + c + 1)
                                    mm = pe.matmul(g.bank[5 + t][:, 0:D], hT[:, c, t * P:(t + 1) * P], w2[:, j, c],
                                                   start=False, stop=(c == FC - 1))
                                mm.then_inc(yp, 1)
                            pe.wait_ge(done, e + 1)

                @block.scalar
                def _(act):
                    with act.Fori(0, E // 2) as pair:
                        for j in range(2):
                            e = 2 * pair + j
                            for c in range(FC):
                                act.wait_ge(hp, FC * e + c + 1)
                                act.activation(hT[:, c], g.bank[1 + c % 4][:, 0:CAP], ACT.Identity,
                                               bias=b1[:, j, c:c + 1]).then_inc(hv, 1)
                            act.wait_ge(done, e + 1)
                            act.dma_start(back[ds(e * CAP, CAP), :].rearrange("(t p) d -> p t d", p=P), yt[:, j])\
                               .then_inc(so[j], 16)
                            act.wait_ge(so[j], 16 * pair + 16)

                @block.vector
                def _(v):
                    with v.Fori(0, E // 2) as pair:
                        for j in range(2):
                            e = 2 * pair + j
                            v.wait_ge(tn, e + 1)
                            v.tensor_copy(xT[:].rearrange("p k n -> p (k n)"), g.bank[0][:]).then_inc(tc2, 1)
                            v.wait_ge(hv, FC * e + FC)
                            for t in range(2):
                                v.wait_ge(yp, 2 * e + t + 1)
                                o = v.tensor_copy(yt[:, j, t], g.bank[5 + t][:, 0:D])
                            o.then_inc(done, 1)

            got = sb("got", [P, D])
            gs = sb("gs", [P, D])
            fcol = sb("fcol", [P, 1], U32)
            gh, gt2, gp, gv = (g.sem("xg_" + n) for n in ("held", "fetched", "turned", "step"))
            with nc.Block() as block:
                @block.gpsimd
                def _(po):
                    with po.Fori(0, TT) as t:
                        po.wait_ge(gv, 3 * t + 1)
                        hold_pool(g, po).then_inc(gh, 1)
                        po.indirect_dma_start(got[:], None, back, bass.IndirectOffsetOnAxis(ap=fcol[:, 0:1], axis=0))\
                          .then_inc(gt2, 16)
                        po.wait_ge(gh, t + 1)

                @block.tensor
                def _(pe):
                    with pe.Fori(0, TT) as t:
                        pe.wait_ge(gv, 3 * t + 2)
                        for k in range(KD):
                            mm = pe.transpose(g.bank[0][:, k * P:(k + 1) * P], gs[:, k * P:(k + 1) * P], ident)
                        mm.then_inc(gp, 1)

                @block.vector
                def _(v):
                    with v.Fori(0, TT) as t:
                        v.tensor_copy(fcol[:], fetch[:, ds(t, 1)]).then_inc(gv, 1)
                        v.wait_ge(gt2, 16 * t + 16)
                        v.tensor_scalar(gs[:], got[:], gate[:, ds(t, 1)], None, ALU.mult).then_inc(gv, 1)
                        v.wait_ge(gp, t + 1)
                        y = g.XN[:, :, ds(t * P, P)]
                        v.tensor_tensor(y, g.bank[0][:, 0:D].rearrange("p (k n) -> p k n", k=KD), y, ALU.add)\
                         .then_inc(gv, 1)
                        v.wait_ge(gv, 3 * t + 3)
        layer_norm_phase(g, "nxl", src=g.XN, dst=g.X, gain=gain, shift=shift, resid=g.X)


HOST_T = ("L1_xattn_w_qkv", "L1_xattn_w_proj", "L1_ffn_router_w", "L3_xattn_W_src", "L3_xattn_W_tgt", "L3_xattn_W_out",
          "L3_ffn_in_proj_w", "L3_ffn_out_proj_w")


def kernel(**inputs):
    import numpy as _np
    import concourse.bacc as _bacc
    from concourse import mybir as _mybir
    from concourse.bass_utils import run_bass_kernel_spmd as _run

    nc = _bacc.Bacc("TRN2", target_bir_lowering=False, num_devices=1)
    a = {k: _np.asarray(v) for k, v in inputs.items()}
    x = a.pop("x").reshape(T, D)
    c = a.pop("ctx_2048").reshape(T, DC)
    lay = {"x": _np.ascontiguousarray(x.T), "ctx_tok": _np.ascontiguousarray(c), "ctx": _np.ascontiguousarray(c.T)}
    for k, v in a.items():
        if k in HOST_T or k == "L0_xattn_W_in":
            v = v.T
        if v.dtype == _np.bool_:
            v = v.view(_np.int32)
        if v.ndim == 0:
            v = v.reshape(1)
        lay[k] = _np.ascontiguousarray(v)
        if v.ndim == 1 and v.size % P == 0:
            lay[k + "_col"] = _np.ascontiguousarray(v.reshape(-1, P).T)
    lay["L2_null_key"] = _np.ascontiguousarray(_np.tile(a["L2_xattn_null_kv"][0][:, None], (1, 8)))
    lay["mask_col"] = _np.ascontiguousarray(a["mask_BxS2_fk1"].reshape(-1, P).T)
    lay["L3_b1_col"] = _np.ascontiguousarray(a["L3_ffn_b1"].reshape(8, -1, P).transpose(0, 2, 1)).reshape(8 * P, -1)
    lay["L3_ffn_w1"] = a["L3_ffn_w1"].reshape(8 * D, -1)
    lay["L3_ffn_w2"] = a["L3_ffn_w2"].reshape(-1, D)
    lay["L0_info_col"] = _np.ascontiguousarray(a["L0_ffn_g_info"][0, 0].reshape(-1, P).T)
    lay["const"] = shape_constants()[1]
    A = {k: nc.dram_tensor("in_" + k, v.shape, _mybir.dt.from_np(v.dtype), kind="ExternalInput").ap()
         for k, v in lay.items()}
    o = nc.dram_tensor("out_x", (D, T), F32, kind="ExternalOutput").ap()
    build(nc, A, o)
    r = _run(nc, [{"in_" + k: v for k, v in lay.items()}], core_ids=[0])
    return _np.ascontiguousarray(r.results[0]["out_x"].T).reshape(B, N, D)
```
